# Optimizing a Trainium2 kernel written in Bass

```python
import numpy as np
import jax
import jax.numpy as jnp

def _softmax(x, axis=-1):
    return jax.nn.softmax(x, axis=axis)

def _gelu(x):
    return jax.nn.gelu(x, approximate=True)

def _silu(x):
    return jax.nn.silu(x)

def _sigmoid(x):
    return jax.nn.sigmoid(x)

def _layernorm(x, axis=-1, eps=1e-05):
    m = jnp.mean(x, axis=axis, keepdims=True)
    v = jnp.var(x, axis=axis, keepdims=True)
    return (x - m) / jnp.sqrt(v + eps)

def _scatter_add(tgt, idx, src, axis=0):
    return tgt.at[idx].add(src)

def _segment_sum(src, seg, n):
    return jax.ops.segment_sum(src, seg, n)
kernel_name = 'mk_gnn_resnorm_d1_gnn_r8_1e75c5'

def setup_inputs(seed: int=0):
    np.random.seed(seed)
    _w = jnp.asarray

    def _rec_inputs():
        import jax
        import jax.numpy as jnp
        _gk = jax.random.key(seed)
        x = -0.000202 + 1 * jax.random.normal(jax.random.fold_in(_gk, 1), (6250, 128), jnp.float32)
        _s = jax.random.randint(jax.random.fold_in(_gk, 2), (50000,), 0, 6250, jnp.int32)
        _d = jax.random.randint(jax.random.fold_in(_gk, 3), (50000,), 0, 6250, jnp.int32)
        _loop = jnp.arange(6250, dtype=jnp.int32)
        src = jnp.concatenate([_s, _d, _loop])
        dst = jnp.concatenate([_d, _s, _loop])
        _o = jnp.argsort(dst, stable=True)
        src = src[_o]
        dst = dst[_o]
        edge_attr_128 = -4.21973e-05 + 0.999841 * jax.random.normal(jax.random.fold_in(_gk, 11), (106250, 128), jnp.float32)
        return (x, src, dst, edge_attr_128)
    x, src, dst, edge_attr_128 = _rec_inputs()

    def _L0_gnn_setup():
        import jax, jax.numpy as jnp
        import numpy as np
        N_NODES = 6250
        N_EDGES = 75000
        F = 128
        LOG2 = np.float32(np.log(2.0))

        def shifted_softplus(x):
            return jax.nn.softplus(x) - LOG2
        key = jax.random.key(seed)
        k1, k2, k3, k4, k5 = jax.random.split(key, 5)
        nodes = jax.random.normal(k1, (N_NODES, F), dtype=jnp.float32)
        edges = jax.random.normal(k2, (N_EDGES, F), dtype=jnp.float32)
        edge_index = jax.random.randint(k3, (2, N_EDGES), 0, N_NODES, dtype=jnp.int32)
        W1 = jax.random.normal(k4, (F, F), dtype=jnp.float32) * np.float32(1.0 / np.sqrt(F))
        W2 = jax.random.normal(k5, (F, F), dtype=jnp.float32) * np.float32(1.0 / np.sqrt(F))
        b1 = jnp.zeros((F,), dtype=jnp.float32)
        b2 = jnp.zeros((F,), dtype=jnp.float32)
        return {'nodes': nodes, 'edges': edges, 'edge_index': edge_index, 'W1': W1, 'b1': b1, 'W2': W2, 'b2': b2}
    _L0_gnn_all = _L0_gnn_setup()
    _L0_gnn_in = {k: v for k, v in _L0_gnn_all.items() if k in ('W1', 'b1', 'W2', 'b2')}
    del _L0_gnn_all
    return {'x': x, 'src': src, 'dst': dst, 'edge_attr_128': edge_attr_128, 'L0_gnn_W1': _L0_gnn_in['W1'], 'L0_gnn_b1': _L0_gnn_in['b1'], 'L0_gnn_W2': _L0_gnn_in['W2'], 'L0_gnn_b2': _L0_gnn_in['b2']}

def reference(x, src, dst, edge_attr_128, L0_gnn_W1, L0_gnn_b1, L0_gnn_W2, L0_gnn_b2):
    import jax
    import jax.numpy as jnp

    def _L0_gnn_ref(nodes, edges, edge_index, W1, b1, W2, b2):
        import jax, jax.numpy as jnp
        import numpy as np
        N_NODES = 6250
        N_EDGES = 75000
        F = 128
        LOG2 = np.float32(np.log(2.0))

        def shifted_softplus(x):
            return jax.nn.softplus(x) - LOG2
        x = shifted_softplus(edges @ W1 + b1)
        x = x @ W2 + b2
        receiver = edge_index[0]
        sender = edge_index[1]
        msg = nodes[sender] * x
        out = jax.ops.segment_sum(msg, receiver, num_segments=nodes.shape[0])
        return out
    edge_index = jnp.stack([src, dst])
    x = _layernorm(x + _L0_gnn_ref(x, edge_attr_128, edge_index, L0_gnn_W1, L0_gnn_b1, L0_gnn_W2, L0_gnn_b2), axis=-1)
    return x

_drawn_inputs = setup_inputs


def setup_inputs(seed=0):
    import zlib

    import numpy as np

    out = dict(_drawn_inputs(seed))
    spreads = {'L0_gnn_b1': (0.0, 0.1), 'L0_gnn_b2': (0.0, 0.1)}
    factors = {}
    for name, (base, spread) in spreads.items():
        noise = np.random.default_rng([zlib.crc32(name.encode()), seed]).standard_normal(out[name].shape)
        drawn = base * np.exp(spread * noise) if base else spread * noise
        out[name] = jnp.asarray(drawn.astype(out[name].dtype))
    for name, factor in factors.items():
        out[name] = (out[name] * factor).astype(out[name].dtype)
    return out
```

```python
import math
from contextlib import ExitStack

import numpy as np

import concourse.bass as bass
from concourse import mybir

P = 128
TILES = 4
GROUP = P * TILES
DEPTH = 4
LN2 = math.log(2.0)
EPS = 1e-5
SPLITS = 3
CLAMP = 20.0


def gnn_program(nc, x, src, dst, edge, w1, b1, w2, b2, out):
    fp32, bf16 = mybir.dt.float32, mybir.dt.bfloat16
    i32, u16 = mybir.dt.int32, mybir.dt.uint16
    ALU, ACT, AX = mybir.AluOpType, mybir.ActivationFunctionType, mybir.AxisListType

    nodes, feat = x.shape
    edges = edge.shape[0]
    assert feat == P
    groups = -(-edges // GROUP)
    whole = edges // GROUP
    assert groups == whole + 1 and groups % DEPTH == 0
    last_start = edges - GROUP
    repeated = whole * GROUP - last_start
    trash_repeated = nodes
    trash = nodes + 1
    table_rows = -(-(nodes + P + 1) // P) * P
    max_base = nodes - P

    node_rows = nodes // P
    tail = nodes - P * node_rows
    x_chunk = 8
    chunks = node_rows // x_chunk
    assert chunks * x_chunk == node_rows

    second = whole - P
    second_pieces = [(0, 64), (64, second - 64)]

    ctx = ExitStack()
    with ctx:
        def sb(name, shape, dtype):
            return ctx.enter_context(nc.sbuf_tensor(name, shape, dtype))

        def bank(name):
            return ctx.enter_context(nc.psum_tensor(name, [P, GROUP], fp32))

        def sem(name):
            return ctx.enter_context(nc.semaphore(name))

        def sems(name, n):
            return [sem(f"{name}{k}") for k in range(n)]

        tables = [nc.dram_tensor(f"table{q}", (table_rows, feat), fp32, kind="Internal").ap()
                  for q in range(TILES)]
        ids = nc.dram_tensor("ids", (groups, 2, GROUP), u16, kind="Internal").ap()
        bases = nc.dram_tensor("bases", (groups, 1), i32, kind="Internal").ap()
        x_parts = nc.dram_tensor("x_parts", (nodes, SPLITS * feat), bf16, kind="Internal").ap()

        ident = sb("ident", [P, P], fp32)
        lower = sb("lower", [P, P], fp32)
        ones = sb("ones", [P, P], bf16)
        ones_col = sb("ones_col", [P, 1], fp32)
        half = sb("half", [P, 1], fp32)
        eps = sb("eps", [P, 1], fp32)
        lane = sb("lane", [P, 1], fp32)
        trash_col = sb("trash_col", [P, 1], fp32)
        zeros = sb("zeros", [P, table_rows], fp32)
        w1_sb = sb("w1_sb", [P, P], fp32)
        w2_sb = sb("w2_sb", [P, P], fp32)
        b1_col = sb("b1_col", [P, 1], fp32)
        b1_shifted = sb("b1_shifted", [P, 1], fp32)
        b2_bc = sb("b2_bc", [P, P], fp32)
        b2_part = sb("b2_part", [P, SPLITS, P], bf16)
        b2_rest = sb("b2_rest", [P, SPLITS, P], fp32)
        b2_sum = sb("b2_sum", [P, 2, P], bf16)
        b2_rows = sb("b2_rows", [P, TILES, P], bf16)

        id_in = [sb(f"id_in{k}", [n, 2, GROUP], i32) for k, n in enumerate((P, second, 1))]
        id_out = [sb(f"id_out{k}", [n, 2, GROUP], u16) for k, n in enumerate((P, second, 1))]
        lo = sb("lo", [P, 3], fp32)
        hi = sb("hi", [P, 3], fp32)
        base_f = sb("base_f", [P, 3], fp32)
        base_i = sb("base_i", [P, 3], i32)
        span = sb("span", [P, 3], fp32)
        outside = sb("outside", [P, 3], fp32)
        outside_any = sb("outside_any", [P, 1], fp32)
        flag = sb("flag", [1, 1], i32)
        base_row = sb("base_row", [1, groups], i32)
        base_bc = sb("base_bc", [P, groups], i32)
        window_node = sb("window_node", [P, groups], fp32)

        x_sb = sb("x_sb", [P, 2, x_chunk, feat], fp32)
        x_rest = sb("x_rest", [P, 2, x_chunk, feat], fp32)
        x_split = sb("x_split", [P, 2, x_chunk, SPLITS, feat], bf16)

        edge_sb = sb("edge_sb", [P, DEPTH, TILES, feat], fp32)
        edge_t = sb("edge_t", [P, 2, GROUP], fp32)
        id_rows = sb("id_rows", [P, DEPTH, 2, GROUP], u16)
        id_cols = sb("id_cols", [P, DEPTH, 2, TILES], u16)
        window = sb("window", [P, DEPTH, SPLITS, feat], bf16)
        onehot = sb("onehot", [P, 2, GROUP], bf16)
        dst_idx = sb("dst_idx", [P, DEPTH, TILES], i32)
        src_f = sb("src_f", [P, DEPTH, TILES], fp32)
        same = sb("same", [P, 2, TILES, P], fp32)
        n_same = sb("n_same", [P, DEPTH, TILES], fp32)
        to_trash = sb("to_trash", [P, DEPTH, TILES], fp32)
        row_idx = sb("row_idx", [P, DEPTH, TILES], i32)
        clamped = sb("clamped", [P, 2, GROUP], fp32)
        soft = sb("soft", [P, 2, GROUP], fp32)
        x_dst = sb("x_dst", [P, DEPTH, GROUP], fp32)
        msg = sb("msg", [P, 2, GROUP], fp32)
        summed = sb("summed", [P, DEPTH, GROUP], fp32)

        FIN = 3
        part_sb = sb("part_sb", [P, FIN, TILES, x_chunk * feat], fp32)
        stats = sb("stats", [P, FIN, x_chunk, 6], fp32)
        mean_var = sb("mean_var", [P, FIN, x_chunk, 2], fp32)
        std = sb("std", [P, FIN, x_chunk], fp32)
        rstd = sb("rstd", [P, FIN, x_chunk], fp32)

        ps_t = [bank(f"ps_t{k}") for k in range(2)]
        ps_h = [bank(f"ps_h{k}") for k in range(2)]
        ps_w = [bank(f"ps_w{k}") for k in range(2)]
        ps_x = bank("ps_x")
        ps_c = bank("ps_c")

        weights_in = sem("weights_in")
        ids_in = sems("ids_in", 3)
        pool_const = sem("pool_const")
        dve_const = sem("dve_const")
        prep = sem("prep")
        ids_ready = sem("ids_ready")
        ids_saved = sem("ids_saved")
        outside_ready = sem("outside_ready")
        flag_sum = sem("flag_sum")
        flag_ready = sem("flag_ready")
        base_row_in = sem("base_row_in")
        base_bc_in = sem("base_bc_in")
        window_node_ready = sem("window_node_ready")
        x_in = sems("x_in", 2)
        x_hi = sem("x_hi")
        x_rest1 = sem("x_rest1")
        x_mid = sem("x_mid")
        x_lo = sem("x_lo")
        x_saved = sems("x_saved", 2)
        tables_set = sem("tables_set")
        edge_in = sems("edge_in", DEPTH)
        rows_in = sems("rows_in", DEPTH)
        cols_in = sems("cols_in", DEPTH)
        window_in = sems("window_in", DEPTH)
        gathered = sems("gathered", DEPTH)
        added = sems("added", TILES)
        transposed = sem("transposed")
        edge_t_ready = sem("edge_t_ready")
        h_ready = sem("h_ready")
        clamped_ready = sem("clamped_ready")
        exp_done = sem("exp_done")
        log_ready = sem("log_ready")
        soft_ready = sem("soft_ready")
        onehot_ready = sem("onehot_ready")
        x_dst_summed = sem("x_dst_summed")
        x_dst_ready = sem("x_dst_ready")
        w_ready = sem("w_ready")
        msg_ready = sem("msg_ready")
        src_f_ready = sem("src_f_ready")
        same_ready = sem("same_ready")
        to_trash_ready = sem("to_trash_ready")
        row_idx_ready = sem("row_idx_ready")
        comb_ready = sem("comb_ready")
        summed_ready = sem("summed_ready")
        gathers_started = sem("gathers_started")
        table_free = sem("table_free")
        part_in = sems("part_in", FIN)
        pair01 = sem("pair01")
        pair23 = sem("pair23")
        y_ready = sem("y_ready")
        stats_ready = sem("stats_ready")
        mean_var_ready = sem("mean_var_ready")
        std_ready = sem("std_ready")
        rstd_ready = sem("rstd_ready")
        norm_ready = sem("norm_ready")
        out_saved = sems("out_saved", FIN)

        block = ctx.enter_context(nc.Block())

        def at(rnd, off):
            return rnd * DEPTH + off, rnd + off // DEPTH, off % DEPTH

        def for_groups(eng, stages):
            late = max(k for k, _ in stages)
            first, end = 2, groups // DEPTH - 1

            def peeled(s):
                for k, stage in stages:
                    if 0 <= s - k < groups:
                        stage(s - k, (s - k) // DEPTH, (s - k) % DEPTH)

            for s in range(first * DEPTH):
                peeled(s)
            with eng.Fori(first, end) as rnd:
                for u in range(DEPTH):
                    for k, stage in stages:
                        stage(*at(rnd, u - k))
            for s in range(end * DEPTH, groups + late):
                peeled(s)

        def reaches(g, n):
            return not isinstance(g, int) or g >= n

        def by_flag(eng, sorted_path, general_path):
            eng.wait_ge(flag_ready, 1)
            value = eng.value_load(flag[0:1, 0:1], min_val=0, max_val=1)
            with eng.If(value == 0):
                sorted_path()
            with eng.Else():
                general_path()

        def node_views(dram, c):
            if c == chunks:
                return dram[P * node_rows:nodes, :], tail, 1
            main = dram[0:P * node_rows, :].rearrange("(p r) f -> p r f", r=node_rows)
            return (main[:, c * x_chunk:(c + 1) * x_chunk, :].rearrange("p r f -> p (r f)"),
                    P, x_chunk)

        @block.sync
        def _(sp):
            for k, g0, n in ((0, 0, P), (1, P, second), (2, None, 1)):
                pieces = second_pieces if k == 1 else [(0, n)]
                for p0, m in pieces:
                    for j, a in ((0, dst), (1, src)):
                        if k == 2:
                            view = a[last_start:edges].rearrange("(p e) -> p e", p=1)
                        else:
                            e0 = (g0 + p0) * GROUP
                            view = a[e0:e0 + m * GROUP].rearrange("(p e) -> p e", p=m)
                        sp.dma_start(id_in[k][p0:p0 + m, j, :], view).then_inc(ids_in[k], 16)

            def load_x(c):
                if c >= 2:
                    sp.wait_ge(x_rest1, c - 1)
                view, n, r = node_views(x, c)
                sp.dma_start(x_sb[0:n, c % 2, 0:r, :].rearrange("p r f -> p (r f)"),
                             view).then_inc(x_in[c % 2], 16)

            def save_x(c):
                sp.wait_ge(x_lo, c + 1)
                sp.wait_ge(x_mid, c + 1)
                if c == chunks:
                    view, n, r = x_parts[P * node_rows:nodes, :], tail, 1
                else:
                    main = x_parts[0:P * node_rows, :].rearrange("(p r) f -> p r f", r=node_rows)
                    view = main[:, c * x_chunk:(c + 1) * x_chunk, :].rearrange("p r f -> p (r f)")
                    n, r = P, x_chunk
                sp.dma_start(view, x_split[0:n, c % 2, 0:r, :, :].rearrange("p r k f -> p (r k f)")
                             ).then_inc(x_saved[c % 2], 16)

            load_x(0)
            load_x(1)
            sp.dma_start(w1_sb[:, :], w1).then_inc(weights_in, 16)
            sp.dma_start(w2_sb[:, :], w2).then_inc(weights_in, 16)
            sp.dma_start(b1_col[:, :], b1.rearrange("(p o) -> p o", o=1)).then_inc(weights_in, 16)
            sp.dma_start(b2_bc[:, :], b2.rearrange("(o f) -> o f", o=1).broadcast_to([P, feat])
                         ).then_inc(weights_in, 16)
            saved = 0
            for k, g0, n in ((0, 0, P), (1, P, second), (2, whole, 1)):
                sp.wait_ge(ids_ready, k + 1)
                for p0, m in (second_pieces if k == 1 else [(0, n)]):
                    sp.dma_start(ids[g0 + p0:g0 + p0 + m, :, :].rearrange("g j e -> g (j e)"),
                                 id_out[k][p0:p0 + m, :, :].rearrange("g j e -> g (j e)")
                                 ).then_inc(ids_saved, 16)
                    sp.dma_start(bases[g0 + p0:g0 + p0 + m, :], base_i[p0:p0 + m, k:k + 1]
                                 ).then_inc(ids_saved, 16)
                    saved += 32
            sp.wait_ge(ids_saved, saved)
            sp.dma_start(base_row[:, :], bases.rearrange("g o -> o g")).then_inc(base_row_in, 16)
            sp.dma_start(base_bc[:, :], bases.rearrange("g o -> o g").broadcast_to([P, groups])
                         ).then_inc(base_bc_in, 16)
            for c in range(chunks + 1):
                save_x(c)
                if c + 2 <= chunks:
                    load_x(c + 2)
            sp.dma_start(tables[0][0:nodes, :].rearrange("(a b) f -> a (b f)", a=125),
                         x.rearrange("(a b) f -> a (b f)", a=125)).then_inc(tables_set, 16)
            sp.wait_ge(pool_const, 4)
            extra = table_rows - nodes
            sp.dma_start(tables[0][nodes:table_rows, :].rearrange("(p r) f -> p (r f)", r=2),
                         zeros[0:extra // 2, 0:2 * feat]).then_inc(tables_set, 16)
            for q in range(1, TILES):
                sp.dma_start(tables[q].rearrange("(p r) f -> p (r f)", p=P), zeros[:, :]
                             ).then_inc(tables_set, 16)
            sp.wait_ge(x_saved[0], 16 * ((chunks + 2) // 2))
            sp.wait_ge(x_saved[1], 16 * ((chunks + 1) // 2))
            sp.wait_ge(base_row_in, 16)

            def start_of(g):
                return last_start if isinstance(g, int) and g == whole else g * GROUP

            def load_edges(g, rnd, b):
                if reaches(g, DEPTH):
                    sp.wait_ge(transposed, g - DEPTH + 1)
                sp.dma_start(edge_sb[:, b, :, :].rearrange("p q f -> p (q f)"),
                             edge[bass.ds(start_of(g), GROUP), :]
                             .rearrange("(p q) f -> p (q f)", q=TILES)).then_inc(edge_in[b], 16)

            def load_ids(g, rnd, b):
                if reaches(g, DEPTH):
                    sp.wait_ge(onehot_ready, g - DEPTH + 1)
                    sp.wait_ge(row_idx_ready, g - DEPTH + 1)
                group = ids[bass.ds(g, 1), :, :]
                sp.dma_start(id_rows[:, b, :, :].rearrange("p j e -> p (j e)"),
                             group.rearrange("g j e -> g (j e)").broadcast_to([P, 2 * GROUP])
                             ).then_inc(rows_in[b], 16)
                sp.dma_start(id_cols[:, b, :, :],
                             group.rearrange("g j (p q) -> (g p) j q", q=TILES)
                             ).then_inc(cols_in[b], 16)

            def load_window(g, rnd, b):
                base = sp.value_load(base_row[0:1, bass.ds(g, 1)], min_val=0, max_val=max_base)
                if reaches(g, DEPTH):
                    sp.wait_ge(x_dst_summed, g - DEPTH + 1)
                sp.dma_start(window[:, b, :, :].rearrange("p k f -> p (k f)"),
                             x_parts[bass.ds(base, P), :]).then_inc(window_in[b], 16)

            by_flag(sp,
                    lambda: for_groups(sp, [(0, load_edges), (0, load_ids), (0, load_window)]),
                    lambda: for_groups(sp, [(0, load_edges), (0, load_ids)]))

            for q in range(TILES):
                sp.wait_ge(added[q], 16 * groups)
            for c in range(chunks + 1):
                if c >= FIN:
                    sp.wait_ge(out_saved[c % FIN], 16 * (c // FIN))
                for q in range(TILES):
                    view, n, r = node_views(tables[q], c)
                    sp.dma_start(part_sb[0:n, c % FIN, q, 0:r * feat], view
                                 ).then_inc(part_in[c % FIN], 16)
            for f in range(FIN):
                sp.wait_ge(out_saved[f], 16 * ((chunks + FIN - f) // FIN))

        @block.gpsimd
        def _(pool):
            pool.memset(ident[:, :], 0.0).then_inc(pool_const, 1)
            pool.memset(lower[:, :], 1.0).then_inc(pool_const, 1)
            pool.iota(lane[:, :], pattern=[[0, 1]], base=0, channel_multiplier=1,
                      allow_small_or_imprecise_dtypes=True).then_inc(pool_const, 1)
            pool.memset(zeros[:, :], 0.0).then_inc(pool_const, 1)
            pool.wait_ge(pool_const, 4)
            pool.affine_select(out=ident[:, :], in_=ident[:, :], compare_op=ALU.not_equal, fill=1.0,
                               base=0, pattern=[[-1, P]], channel_multiplier=1).then_inc(pool_const, 1)
            pool.affine_select(out=lower[:, :], in_=lower[:, :], compare_op=ALU.is_ge, fill=0.0,
                               base=0, pattern=[[-1, P]], channel_multiplier=1).then_inc(pool_const, 1)
            pool.wait_ge(tables_set, 16 * (TILES + 1))

            def add_rows(g, rnd, b):
                pool.wait_ge(summed_ready, g + 1)
                pool.wait_ge(row_idx_ready, g + 1)
                for q in range(TILES):
                    if reaches(g, 1):
                        pool.wait_ge(added[q], 16 * g)
                        pool.sem_inc(table_free, 1)
                    pool.indirect_dma_start(
                        out=tables[q],
                        out_offset=bass.IndirectOffsetOnAxis(ap=row_idx[:, b, q:q + 1], axis=0),
                        in_=summed[:, b, q * feat:(q + 1) * feat], in_offset=None,
                        compute_op=ALU.add).then_inc(added[q], 16)

            def gather_x(g, rnd, b):
                pool.wait_ge(onehot_ready, g + 1)
                if reaches(g, DEPTH):
                    pool.wait_ge(msg_ready, g - DEPTH + 1)
                pool.sem_inc(gathers_started, 1)
                for q in range(TILES):
                    pool.indirect_dma_start(
                        out=x_dst[:, b, q * feat:(q + 1) * feat], out_offset=None, in_=x,
                        in_offset=bass.IndirectOffsetOnAxis(ap=dst_idx[:, b, q:q + 1], axis=0)
                    ).then_inc(gathered[b], 16)

            by_flag(pool,
                    lambda: for_groups(pool, [(0, add_rows)]),
                    lambda: for_groups(pool, [(0, gather_x), (2, add_rows)]))

            for c in range(chunks + 1):
                n, r = (tail, 1) if c == chunks else (P, x_chunk)
                pool.wait_ge(part_in[c % FIN], 16 * TILES * (c // FIN + 1))
                two, three = (part_sb[0:n, c % FIN, q, 0:r * feat] for q in (2, 3))
                pool.tensor_tensor(two, two, three, ALU.add).then_inc(pair23, 1)

        @block.scalar
        def _(act):
            for c in range(chunks + 1):
                n, r = (tail, 1) if c == chunks else (P, x_chunk)
                act.wait_ge(x_in[c % 2], 16 * (c // 2 + 1))
                if c >= 2:
                    act.wait_ge(x_saved[c % 2], 16 * (c // 2))
                nc.scalar.activation(x_split[0:n, c % 2, 0:r, 0, :], x_sb[0:n, c % 2, 0:r, :],
                                     ACT.Copy).then_inc(x_hi, 1)
                act.wait_ge(x_rest1, c + 1)
                nc.scalar.activation(x_split[0:n, c % 2, 0:r, 1, :], x_rest[0:n, c % 2, 0:r, :],
                                     ACT.Copy).then_inc(x_mid, 1)
            act.wait_ge(dve_const, 4)
            nc.scalar.preload_act_table_set("natural_log_exp_and_others")

            def copy_edge_t(g, rnd, b):
                act.wait_ge(transposed, g + 1)
                if reaches(g, 2):
                    act.wait_ge(h_ready, g - 1)
                nc.scalar.activation(edge_t[:, b % 2, :], ps_t[b % 2][:, :], ACT.Copy
                                     ).then_inc(edge_t_ready, 1)

            def copy_summed(g, rnd, b):
                act.wait_ge(comb_ready, g + 1)
                if reaches(g, DEPTH):
                    act.wait_ge(table_free, TILES * (g - DEPTH + 1))
                nc.scalar.activation(summed[:, b, :], ps_c[:, :], ACT.Copy).then_inc(summed_ready, 1)

            def exp_log(g, rnd, b):
                act.wait_ge(clamped_ready, g + 1)
                nc.scalar.activation(clamped[:, b % 2, :], clamped[:, b % 2, :], ACT.Exp
                                     ).then_inc(exp_done, 1)
                act.wait_ge(exp_done, g + 1)
                nc.scalar.activation(clamped[:, b % 2, :], clamped[:, b % 2, :], ACT.Ln,
                                     bias=half[:, 0:1], scale=0.5).then_inc(log_ready, 1)

            def copy_x_dst(g, rnd, b):
                act.wait_ge(x_dst_summed, g + 1)
                if reaches(g, DEPTH):
                    act.wait_ge(msg_ready, g - DEPTH + 1)
                nc.scalar.activation(x_dst[:, b, :], ps_x[:, :], ACT.Copy).then_inc(x_dst_ready, 1)

            by_flag(act,
                    lambda: for_groups(act, [(0, copy_edge_t), (1, exp_log), (2, copy_x_dst),
                                             (3, copy_summed)]),
                    lambda: for_groups(act, [(0, copy_edge_t), (1, exp_log), (3, copy_summed)]))

            for c in range(chunks + 1):
                n, r = (tail, 1) if c == chunks else (P, x_chunk)
                act.wait_ge(mean_var_ready, c + 1)
                nc.scalar.activation(std[0:n, c % FIN, 0:r], mean_var[0:n, c % FIN, 0:r, 1],
                                     ACT.Sqrt, bias=eps[0:n, 0:1]).then_inc(std_ready, 1)
                act.wait_ge(norm_ready, c + 1)
                view, n, r = node_views(out, c)
                act.dma_start(view, part_sb[0:n, c % FIN, 0, 0:r * feat]).then_inc(out_saved[c % FIN], 16)

        @block.vector
        def _(dve):
            done = [0]

            def then(ins):
                done[0] += 1
                ins.then_inc(prep, 1)
                dve.wait_ge(prep, done[0])

            nc.vector.memset(ones[:, :], 1.0).then_inc(dve_const, 1)
            nc.vector.memset(ones_col[:, :], 1.0).then_inc(dve_const, 1)
            nc.vector.memset(half[:, :], 0.5).then_inc(dve_const, 1)
            nc.vector.memset(eps[:, :], EPS).then_inc(dve_const, 1)
            then(nc.vector.memset(outside[:, :], 0.0))
            for k, n in enumerate((P, second, 1)):
                dve.wait_ge(ids_in[k], 64 if k == 1 else 32)
                then(nc.vector.tensor_copy(id_out[k][:, :, :], id_in[k][:, :, :]))
                if k == 2:
                    then(nc.vector.memset(id_out[k][:, 1, 0:repeated], trash_repeated))
                then(nc.vector.tensor_reduce(lo[0:n, k:k + 1], id_in[k][:, 0, :], AX.X, ALU.min))
                then(nc.vector.tensor_reduce(hi[0:n, k:k + 1], id_in[k][:, 0, :], AX.X, ALU.max))
                then(nc.vector.tensor_scalar(base_f[0:n, k:k + 1], lo[0:n, k:k + 1],
                                             float(max_base), None, ALU.min))
                then(nc.vector.tensor_tensor(span[0:n, k:k + 1], hi[0:n, k:k + 1],
                                             base_f[0:n, k:k + 1], ALU.subtract))
                then(nc.vector.tensor_scalar(outside[0:n, k:k + 1], span[0:n, k:k + 1],
                                             float(P - 1), None, ALU.is_gt))
                nc.vector.tensor_copy(base_i[0:n, k:k + 1], base_f[0:n, k:k + 1]).then_inc(ids_ready, 1)
            nc.vector.tensor_reduce(outside_any[:, :], outside[:, :], AX.X, ALU.max
                                    ).then_inc(outside_ready, 1)
            dve.wait_ge(flag_sum, 1)
            nc.vector.tensor_scalar(flag[:, :], ps_c[0:1, 0:1], 1.0, None, ALU.min
                                    ).then_inc(flag_ready, 1)

            dve.wait_ge(pool_const, 6)
            dve.wait_ge(weights_in, 64)
            then(nc.vector.tensor_scalar(trash_col[:, :], lane[:, :], float(trash), None, ALU.add))
            then(nc.vector.tensor_scalar(b1_shifted[:, :], b1_col[:, :], -LN2, None, ALU.add))
            rest = b2_bc[:, :]
            for k in range(SPLITS):
                then(nc.vector.tensor_copy(b2_part[:, k, :], rest))
                then(nc.vector.tensor_tensor(b2_rest[:, k, :], rest, b2_part[:, k, :], ALU.subtract))
                rest = b2_rest[:, k, :]
            then(nc.vector.tensor_scalar(b2_sum[:, 0, :], b2_part[:, 0, :], ident[:, 0:1], None,
                                         ALU.mult))
            then(nc.vector.scalar_tensor_tensor(b2_sum[:, 1, :], b2_part[:, 1, :], ident[:, 1:2],
                                                b2_sum[:, 0, :], ALU.mult, ALU.add))
            for q in range(TILES):
                then(nc.vector.scalar_tensor_tensor(b2_rows[:, q, :], b2_part[:, 2, :],
                                                    ident[:, 2:3], b2_sum[:, 1, :],
                                                    ALU.mult, ALU.add))
            dve.wait_ge(base_bc_in, 16)
            then(nc.vector.tensor_scalar(window_node[:, :], base_bc[:, :], lane[:, 0:1], None, ALU.add))
            nc.vector.memset(half[:, :], 0.5).then_inc(window_node_ready, 1)

            for c in range(chunks + 1):
                n, r = (tail, 1) if c == chunks else (P, x_chunk)
                dve.wait_ge(x_hi, c + 1)
                if c >= 2:
                    dve.wait_ge(x_lo, c - 1)
                nc.vector.tensor_tensor(x_rest[0:n, c % 2, 0:r, :], x_sb[0:n, c % 2, 0:r, :],
                                        x_split[0:n, c % 2, 0:r, 0, :], ALU.subtract
                                        ).then_inc(x_rest1, 1)
                dve.wait_ge(x_mid, c + 1)
                dve.wait_ge(x_rest1, c + 1)
                nc.vector.tensor_tensor(x_split[0:n, c % 2, 0:r, 2, :], x_rest[0:n, c % 2, 0:r, :],
                                        x_split[0:n, c % 2, 0:r, 1, :], ALU.subtract
                                        ).then_inc(x_lo, 1)

            def clamp(g, rnd, b):
                dve.wait_ge(h_ready, g + 1)
                if reaches(g, 2):
                    dve.wait_ge(soft_ready, g - 1)
                nc.vector.tensor_scalar(clamped[:, b % 2, :], ps_h[b % 2][:, :], b1_col[:, 0:1],
                                        CLAMP, ALU.add, ALU.min).then_inc(clamped_ready, 1)

            def make_onehot(g, rnd, b):
                dve.wait_ge(rows_in[b], 16 * (rnd + 1))
                if reaches(g, 2):
                    dve.wait_ge(x_dst_summed, g - 1)
                nc.vector.tensor_scalar(onehot[:, b % 2, :], id_rows[:, b, 0, :],
                                        window_node[:, bass.ds(g, 1)], None, ALU.is_equal
                                        ).then_inc(onehot_ready, 1)

            def make_dst_idx(g, rnd, b):
                dve.wait_ge(cols_in[b], 16 * (rnd + 1))
                if reaches(g, DEPTH):
                    dve.wait_ge(gathered[b], 16 * TILES * rnd)
                nc.vector.tensor_copy(dst_idx[:, b, :], id_cols[:, b, 0, :]).then_inc(onehot_ready, 1)

            def make_same(g, rnd, b):
                dve.wait_ge(cols_in[b], 16 * (rnd + 1))
                nc.vector.tensor_copy(src_f[:, b, :], id_cols[:, b, 1, :]).then_inc(src_f_ready, 1)
                dve.wait_ge(rows_in[b], 16 * (rnd + 1))
                if reaches(g, 2):
                    dve.wait_ge(comb_ready, g - 1)
                dve.wait_ge(src_f_ready, g + 1)
                for q in range(TILES):
                    nc.vector.scalar_tensor_tensor(
                        same[:, b % 2, q, :], id_rows[:, b, 1, q::TILES], src_f[:, b, q:q + 1],
                        lower[:, :], ALU.is_equal, ALU.mult,
                        accum_out=n_same[:, b, q:q + 1]).then_inc(same_ready, 1)
                dve.wait_ge(same_ready, TILES * (g + 1))
                nc.vector.tensor_scalar(to_trash[:, b, :], n_same[:, b, :], 1.5, trash_col[:, 0:1],
                                        ALU.is_gt, ALU.mult).then_inc(to_trash_ready, 1)
                if reaches(g, DEPTH):
                    dve.wait_ge(table_free, TILES * (g - DEPTH + 1))
                dve.wait_ge(to_trash_ready, g + 1)
                nc.vector.tensor_tensor(row_idx[:, b, :], to_trash[:, b, :], src_f[:, b, :], ALU.max
                                        ).then_inc(row_idx_ready, 1)

            def softplus(g, rnd, b):
                dve.wait_ge(log_ready, g + 1)
                nc.vector.scalar_tensor_tensor(soft[:, b % 2, :], ps_h[b % 2][:, :],
                                               b1_shifted[:, 0:1], clamped[:, b % 2, :],
                                               ALU.add, ALU.max).then_inc(soft_ready, 1)

            def multiply(g, rnd, b):
                dve.wait_ge(w_ready, g + 1)
                nc.vector.tensor_tensor(msg[:, b % 2, :], ps_w[b % 2][:, :], x_dst[:, b, :], ALU.mult
                                        ).then_inc(msg_ready, 1)

            def multiply_summed(g, rnd, b):
                dve.wait_ge(x_dst_ready, g + 1)
                multiply(g, rnd, b)

            def multiply_gathered(g, rnd, b):
                dve.wait_ge(gathered[b], 16 * TILES * (rnd + 1))
                multiply(g, rnd, b)

            by_flag(dve,
                    lambda: for_groups(dve, [(3, multiply_summed), (1, clamp), (2, make_same),
                                             (1, make_onehot), (1, softplus)]),
                    lambda: for_groups(dve, [(3, multiply_gathered), (1, clamp), (2, make_same),
                                             (1, make_dst_idx), (1, softplus)]))

            for c in range(chunks + 1):
                n, r = (tail, 1) if c == chunks else (P, x_chunk)
                f = c % FIN
                zero, one, two = (part_sb[0:n, f, q, 0:r * feat] for q in range(3))
                dve.wait_ge(part_in[f], 16 * TILES * (c // FIN + 1))
                nc.vector.tensor_tensor(zero, zero, one, ALU.add).then_inc(pair01, 1)
                dve.wait_ge(pair01, c + 1)
                dve.wait_ge(pair23, c + 1)
                nc.vector.tensor_tensor(zero, zero, two, ALU.add).then_inc(y_ready, 1)
                dve.wait_ge(y_ready, c + 1)
                for k in range(r):
                    last = nc.vector.bn_stats(stats[0:n, f, k, :],
                                              part_sb[0:n, f, 0, k * feat:(k + 1) * feat])
                last.then_inc(stats_ready, 1)
                dve.wait_ge(stats_ready, c + 1)
                for k in range(r):
                    last = nc.vector.bn_aggr(mean_var[0:n, f, k, :], stats[0:n, f, k, :])
                last.then_inc(mean_var_ready, 1)
                dve.wait_ge(std_ready, c + 1)
                nc.vector.reciprocal(rstd[0:n, f, 0:r], std[0:n, f, 0:r]).then_inc(rstd_ready, 1)
                dve.wait_ge(rstd_ready, c + 1)
                for k in range(r):
                    row = part_sb[0:n, f, 0, k * feat:(k + 1) * feat]
                    last = nc.vector.tensor_scalar(row, row, mean_var[0:n, f, k, 0:1],
                                                   rstd[0:n, f, k:k + 1], ALU.subtract, ALU.mult)
                last.then_inc(norm_ready, 1)

        @block.tensor
        def _(pe):
            pe.wait_ge(dve_const, 4)
            pe.wait_ge(outside_ready, 1)
            nc.tensor.matmul(ps_c[0:1, 0:1], outside_any[:, :], ones_col[:, :], start=True, stop=True
                             ).then_inc(flag_sum, 1)
            pe.wait_ge(window_node_ready, 1)

            def transpose(g, rnd, b):
                pe.wait_ge(edge_in[b], 16 * (rnd + 1))
                if reaches(g, 2):
                    pe.wait_ge(edge_t_ready, g - 1)
                for q in range(TILES):
                    last = nc.tensor.transpose(ps_t[b % 2][:, q * P:(q + 1) * P],
                                               edge_sb[:, b, q, :], ident[:, :])
                last.then_inc(transposed, 1)

            def combine(g, rnd, b):
                pe.wait_ge(msg_ready, g + 1)
                pe.wait_ge(row_idx_ready, g + 1)
                if reaches(g, 1):
                    pe.wait_ge(summed_ready, g)
                for q in range(TILES):
                    last = nc.tensor.matmul(ps_c[:, q * P:(q + 1) * P], same[:, b % 2, q, :],
                                            msg[:, b % 2, q * P:(q + 1) * P], start=True, stop=True)
                last.then_inc(comb_ready, 1)

            def layer1(g, rnd, b):
                pe.wait_ge(edge_t_ready, g + 1)
                if reaches(g, 2):
                    pe.wait_ge(soft_ready, g - 1)
                nc.tensor.matmul(ps_h[b % 2][:, :], w1_sb[:, :], edge_t[:, b % 2, :],
                                 start=True, stop=True).then_inc(h_ready, 1)

            def sum_x_dst(g, rnd, b):
                pe.wait_ge(onehot_ready, g + 1)
                pe.wait_ge(window_in[b], 16 * (rnd + 1))
                if reaches(g, 1):
                    pe.wait_ge(x_dst_ready, g)
                for q in range(TILES):
                    for k in range(SPLITS):
                        last = nc.tensor.matmul(ps_x[:, q * P:(q + 1) * P],
                                                onehot[:, b % 2, q::TILES], window[:, b, k, :],
                                                start=(k == 0), stop=(k == SPLITS - 1))
                last.then_inc(x_dst_summed, 1)

            def layer2(g, rnd, b):
                if reaches(g, 2):
                    pe.wait_ge(msg_ready, g - 1)
                nc.tensor.matmul(ps_w[b % 2][:, :], ones[:, :],
                                 b2_rows[:, :, :].rearrange("p q f -> p (q f)"),
                                 start=True, stop=False, skip_group_check=True)
                pe.wait_ge(soft_ready, g + 1)
                for q in range(TILES):
                    last = nc.tensor.matmul(ps_w[b % 2][:, q * P:(q + 1) * P],
                                            soft[:, b % 2, q * P:(q + 1) * P], w2_sb[:, :],
                                            start=False, stop=True, skip_group_check=True)
                last.then_inc(w_ready, 1)

            by_flag(pe,
                    lambda: for_groups(pe, [(0, transpose), (1, layer1), (2, sum_x_dst),
                                            (3, combine), (2, layer2)]),
                    lambda: for_groups(pe, [(0, transpose), (1, layer1), (3, combine),
                                            (2, layer2)]))


_INPUTS = ["x", "src", "dst", "edge_attr_128", "L0_gnn_W1", "L0_gnn_b1", "L0_gnn_W2", "L0_gnn_b2"]


def kernel(**inputs):
    from concourse import bacc
    from concourse.bass_utils import run_bass_kernel_spmd

    nc = bacc.Bacc("TRN2", target_bir_lowering=False, num_devices=1)
    arrays, views = {}, []
    for name in _INPUTS:
        a = np.ascontiguousarray(inputs[name])
        arrays[f"in_{name}"] = a
        views.append(nc.dram_tensor(f"in_{name}", a.shape, mybir.dt.from_np(a.dtype),
                                    kind="ExternalInput").ap())
    shape = np.asarray(inputs["x"]).shape
    views.append(nc.dram_tensor("out", shape, mybir.dt.float32, kind="ExternalOutput").ap())
    gnn_program(nc, *views)
    return run_bass_kernel_spmd(nc, [arrays], core_ids=[0]).results[0]["out"]
```

```python
import math
from contextlib import ExitStack

import numpy as np

import concourse.bass as bass
from concourse import mybir

P = 128
TILES = 4
GROUP = P * TILES
DEPTH = 4
LN2 = math.log(2.0)
EPS = 1e-5
SPLITS = 3
EXACT = 20
EARLY = 2
SAVE_STEP = 5
CLAMP = 20.0


def gnn_program(nc, x, src, dst, edge, w1, b1, w2, b2, out):
    fp32, bf16 = mybir.dt.float32, mybir.dt.bfloat16
    i32, u16 = mybir.dt.int32, mybir.dt.uint16
    ALU, ACT, AX = mybir.AluOpType, mybir.ActivationFunctionType, mybir.AxisListType

    nodes, feat = x.shape
    edges = edge.shape[0]
    assert feat == P
    groups = -(-edges // GROUP)
    whole = edges // GROUP
    assert groups == whole + 1 and groups % DEPTH == 0
    last_start = edges - GROUP
    repeated = whole * GROUP - last_start
    trash_repeated = nodes
    trash = nodes + 1
    table_rows = -(-(nodes + P + 1) // P) * P
    zero_rows = 10
    assert table_rows % (P * zero_rows) == 0
    max_base = nodes - P

    node_rows = nodes // P
    tail = nodes - P * node_rows
    x_chunk = 8
    chunks = node_rows // x_chunk
    assert chunks * x_chunk == node_rows

    second = whole - P
    second_pieces = [(0, 64), (64, second - 64)]

    ctx = ExitStack()
    with ctx:
        def sb(name, shape, dtype):
            return ctx.enter_context(nc.sbuf_tensor(name, shape, dtype))

        def bank(name):
            return ctx.enter_context(nc.psum_tensor(name, [P, GROUP], fp32))

        def sem(name):
            return ctx.enter_context(nc.semaphore(name))

        def sems(name, n):
            return [sem(f"{name}{k}") for k in range(n)]

        tables = [nc.dram_tensor(f"table{q}", (table_rows, feat), fp32, kind="Internal").ap()
                  for q in range(TILES)]
        ids = nc.dram_tensor("ids", (groups, 2, GROUP), u16, kind="Internal").ap()
        x_parts = nc.dram_tensor("x_parts", (nodes, SPLITS * feat), bf16, kind="Internal").ap()

        ident = sb("ident", [P, P], fp32)
        lower = sb("lower", [P, P], fp32)
        ones = sb("ones", [P, P], bf16)
        half = sb("half", [P, 1], fp32)
        eps = sb("eps", [P, 1], fp32)
        lane = sb("lane", [P, 1], fp32)
        trash_col = sb("trash_col", [P, 1], fp32)
        zeros = sb("zeros", [P, zero_rows * feat], fp32)
        ones_f = sb("ones_f", [P, P], fp32)
        w1_sb = sb("w1_sb", [P, P], fp32)
        w2_sb = sb("w2_sb", [P, P], fp32)
        b1_col = sb("b1_col", [P, 1], fp32)
        b1_shifted = sb("b1_shifted", [P, 1], fp32)
        b2_bc = sb("b2_bc", [P, P], fp32)
        b2_part = sb("b2_part", [P, SPLITS, P], bf16)
        b2_rest = sb("b2_rest", [P, SPLITS, P], fp32)
        b2_sum = sb("b2_sum", [P, 2, P], bf16)
        b2_rows = sb("b2_rows", [P, TILES, P], bf16)

        id_in = [sb(f"id_in{k}", [n, 2, GROUP], i32) for k, n in enumerate((P, second, 1))]
        id_out = [sb(f"id_out{k}", [n, 2, GROUP], u16) for k, n in enumerate((P, second, 1))]
        lo = sb("lo", [P, 3], fp32)
        hi = sb("hi", [P, 3], fp32)
        base_f = sb("base_f", [P, 3], fp32)
        base_diag = sb("base_diag", [P, groups], fp32)
        span = sb("span", [P, 3], fp32)
        outside = sb("outside", [P, 3], fp32)
        outside_any = sb("outside_any", [P, 1], fp32)
        flag = sb("flag", [1, 1], i32)
        base_row = sb("base_row", [1, groups], i32)
        window_node = sb("window_node", [P, groups], fp32)

        x_sb = sb("x_sb", [P, chunks + 1, x_chunk * feat], fp32)

        edge_sb = sb("edge_sb", [P, DEPTH, TILES, feat], fp32)
        edge_t = sb("edge_t", [P, 2, GROUP], fp32)
        id_rows = sb("id_rows", [P, DEPTH, 2, GROUP], u16)
        id_cols = sb("id_cols", [P, DEPTH, 2, TILES], u16)
        window = sb("window", [P, DEPTH, SPLITS, feat], bf16)
        window_x = sb("window_x", [P, DEPTH, feat], fp32)
        onehot_f = sb("onehot_f", [P, 2, GROUP], fp32)
        onehot = sb("onehot", [P, 2, GROUP], bf16)
        dst_idx = sb("dst_idx", [P, DEPTH, TILES], i32)
        src_f = sb("src_f", [P, DEPTH, TILES], fp32)
        same = sb("same", [P, 2, TILES, P], fp32)
        n_same = sb("n_same", [P, DEPTH, TILES], fp32)
        to_trash = sb("to_trash", [P, DEPTH, TILES], fp32)
        row_idx = sb("row_idx", [P, DEPTH, TILES], i32)
        clamped = sb("clamped", [P, 2, GROUP], fp32)
        soft = sb("soft", [P, 2, GROUP], fp32)
        x_dst = sb("x_dst", [P, DEPTH, GROUP], fp32)
        msg = sb("msg", [P, 2, GROUP], fp32)
        summed = sb("summed", [P, DEPTH, GROUP], fp32)

        FIN = 8
        ln_rows = 4
        ln_chunks = node_rows // ln_rows
        assert ln_chunks * ln_rows == node_rows
        part_sb = sb("part_sb", [P, FIN, TILES, ln_rows * feat], fp32)
        x_split = (part_sb[:, :, :, :].rearrange("p b t e -> p (b t e)").bitcast(bf16)
                   [:, 0:(node_rows + 1) * SPLITS * feat]
                   .rearrange("p (r k f) -> p r k f", k=SPLITS, f=feat))
        stats = sb("stats", [P, FIN, ln_rows, 6], fp32)
        mean_var = sb("mean_var", [P, FIN, ln_rows, 2], fp32)
        std = sb("std", [P, FIN, ln_rows], fp32)
        rstd = sb("rstd", [P, FIN, ln_rows], fp32)

        ps_t = [bank(f"ps_t{k}") for k in range(2)]
        ps_h = [bank(f"ps_h{k}") for k in range(2)]
        ps_w = [bank(f"ps_w{k}") for k in range(2)]
        ps_x = bank("ps_x")
        ps_c = bank("ps_c")

        weights_in = sem("weights_in")
        ids_in = sems("ids_in", 3)
        pool_const = sem("pool_const")
        dve_const = sem("dve_const")
        prep = sem("prep")
        ids_ready = sem("ids_ready")
        repeated_set = sem("repeated_set")
        ids_saved = sem("ids_saved")
        outside_ready = sem("outside_ready")
        flag_sum = sem("flag_sum")
        flag_ready = sem("flag_ready")
        diag_ready = sem("diag_ready")
        base_sum = sem("base_sum")
        base_row_ready = sem("base_row_ready")
        b2_ready = sem("b2_ready")
        x_in = sems("x_in", chunks + 1)
        x_hi = sem("x_hi")
        x_rest = sem("x_rest")
        x_mid = sem("x_mid")
        x_split_ready = sem("x_split_ready")
        x_saved = sem("x_saved")
        table_set = sems("table_set", TILES)
        edge_in = sems("edge_in", DEPTH)
        rows_in = sems("rows_in", DEPTH)
        cols_in = sems("cols_in", DEPTH)
        window_in = sems("window_in", DEPTH)
        gathered = sems("gathered", DEPTH)
        added = sems("added", TILES)
        transposed = sem("transposed")
        edge_t_ready = sem("edge_t_ready")
        h_ready = sem("h_ready")
        clamped_ready = sem("clamped_ready")
        exp_done = sem("exp_done")
        log_ready = sem("log_ready")
        soft_ready = sem("soft_ready")
        onehot_ready = sem("onehot_ready")
        x_dst_summed = sem("x_dst_summed")
        x_dst_ready = sem("x_dst_ready")
        w_ready = sem("w_ready")
        msg_ready = sem("msg_ready")
        src_f_ready = sem("src_f_ready")
        same_ready = sem("same_ready")
        to_trash_ready = sem("to_trash_ready")
        row_idx_ready = sem("row_idx_ready")
        comb_ready = sem("comb_ready")
        summed_ready = sem("summed_ready")
        gathers_started = sem("gathers_started")
        table_free = sem("table_free")
        part_in = sems("part_in", FIN)
        pair01 = sem("pair01")
        pair23 = sem("pair23")
        y_ready = sem("y_ready")
        stats_ready = sem("stats_ready")
        mean_var_ready = sem("mean_var_ready")
        std_ready = sem("std_ready")
        rstd_ready = sem("rstd_ready")
        norm_ready = sem("norm_ready")
        out_saved = sems("out_saved", FIN)

        block = ctx.enter_context(nc.Block())

        def at(rnd, off):
            return rnd * DEPTH + off, rnd + off // DEPTH, off % DEPTH

        def for_groups(eng, stages):
            late = max(k for k, _ in stages)
            first, end = EXACT // DEPTH + 1, groups // DEPTH - 1

            def peeled(s):
                for k, stage in stages:
                    if 0 <= s - k < groups:
                        stage(s - k, (s - k) // DEPTH, (s - k) % DEPTH)

            for s in range(first * DEPTH):
                peeled(s)
            with eng.Fori(first, end) as rnd:
                for u in range(DEPTH):
                    for k, stage in stages:
                        stage(*at(rnd, u - k))
            for s in range(end * DEPTH, groups + late):
                peeled(s)

        def reaches(g, n):
            return not isinstance(g, int) or g >= n

        def added_before(t, g):
            if isinstance(g, int) and g <= EARLY:
                return 2 * g if t < 2 else 0
            return g + EARLY if t < 2 else g - EARLY

        def exact(g):
            return isinstance(g, int) and g < EXACT

        def by_flag(eng, sorted_path, general_path):
            eng.wait_ge(flag_ready, 1)
            value = eng.value_load(flag[0:1, 0:1], min_val=0, max_val=1)
            with eng.If(value == 0):
                sorted_path()
            with eng.Else():
                general_path()

        def node_views(dram, c, rows=x_chunk):
            if c == node_rows // rows:
                return dram[P * node_rows:nodes, :], tail, 1
            main = dram[0:P * node_rows, :].rearrange("(p r) f -> p r f", r=node_rows)
            return (main[:, c * rows:(c + 1) * rows, :].rearrange("p r f -> p (r f)"), P, rows)

        def ln_size(c):
            return (tail, 1) if c == ln_chunks else (P, ln_rows)

        def zero_block(t, a):
            return tables[t].rearrange("(p a r) f -> a p (r f)", p=P, r=zero_rows)[a]

        zero_blocks = table_rows // (P * zero_rows)
        table_set_by = [16 * (zero_blocks + 0)] * TILES
        table_set_by[0] = 16 * 5

        def x_rows(c):
            n, r = (tail, 1) if c == chunks else (P, x_chunk)
            return x_sb[0:n, c, 0:r * feat].rearrange("p (r f) -> p r f", f=feat)

        def part_rows(c, k):
            n, r = (tail, 1) if c == chunks else (P, x_chunk)
            return x_split[0:n, c * x_chunk:c * x_chunk + r, k, :]

        @block.sync
        def _(sp):
            for k, g0, n in ((0, 0, P), (1, P, second), (2, None, 1)):
                pieces = second_pieces if k == 1 else [(0, n)]
                for p0, m in pieces:
                    for j, a in ((0, dst), (1, src)):
                        if k == 2:
                            view = a[last_start:edges].rearrange("(p e) -> p e", p=1)
                        else:
                            e0 = (g0 + p0) * GROUP
                            view = a[e0:e0 + m * GROUP].rearrange("(p e) -> p e", p=m)
                        sp.dma_start(id_in[k][p0:p0 + m, j, :], view).then_inc(ids_in[k], 16)

            sp.dma_start(w1_sb[:, :], w1).then_inc(weights_in, 16)
            sp.dma_start(w2_sb[:, :], w2).then_inc(weights_in, 16)
            sp.dma_start(b1_col[:, :], b1.rearrange("(p o) -> p o", o=1)).then_inc(weights_in, 16)
            sp.dma_start(b2_bc[:, :], b2.rearrange("(o f) -> o f", o=1).broadcast_to([P, feat])
                         ).then_inc(weights_in, 16)
            def set_x(r0, r1):
                rows = [a[0:P * node_rows, :].rearrange("(p r) f -> p r f", r=node_rows)
                        [:, r0:r1, :].rearrange("p r f -> p (r f)") for a in (tables[0], x)]
                sp.dma_start(*rows).then_inc(table_set[0], 16)

            third = node_rows // 3
            set_x(0, third)
            saved = 0
            for k, g0, n in ((0, 0, P), (1, P, second), (2, whole, 1)):
                sp.wait_ge(ids_ready, k + 1)
                if k == 2:
                    sp.wait_ge(repeated_set, 1)
                for p0, m in (second_pieces if k == 1 else [(0, n)]):
                    sp.dma_start(ids[g0 + p0:g0 + p0 + m, :, :].rearrange("g j e -> g (j e)"),
                                 id_out[k][p0:p0 + m, :, :].rearrange("g j e -> g (j e)")
                                 ).then_inc(ids_saved, 16)
                    saved += 16
            set_x(third, 2 * third)
            set_x(2 * third, node_rows)
            sp.dma_start(tables[0][P * node_rows:nodes, :], x[P * node_rows:nodes, :]
                         ).then_inc(table_set[0], 16)
            sp.wait_ge(dve_const, 5)
            extra = table_rows - nodes
            sp.dma_start(tables[0][nodes:table_rows, :].rearrange("(p r) f -> p (r f)", r=2),
                         zeros[0:extra // 2, 0:2 * feat]).then_inc(table_set[0], 16)
            sp.wait_ge(ids_saved, saved)

            def start_of(g):
                return last_start if isinstance(g, int) and g == whole else g * GROUP

            def load_edges(g, rnd, b):
                if reaches(g, DEPTH):
                    sp.wait_ge(transposed, g - DEPTH + 1)
                sp.dma_start(edge_sb[:, b, :, :].rearrange("p q f -> p (q f)"),
                             edge[bass.ds(start_of(g), GROUP), :]
                             .rearrange("(p q) f -> p (q f)", q=TILES)).then_inc(edge_in[b], 16)

            def load_ids(g, rnd, b):
                if reaches(g, DEPTH):
                    sp.wait_ge(onehot_ready, g - DEPTH + 1)
                    sp.wait_ge(row_idx_ready, g - DEPTH + 1)
                group = ids[bass.ds(g, 1), :, :]
                sp.dma_start(id_rows[:, b, :, :].rearrange("p j e -> p (j e)"),
                             group.rearrange("g j e -> g (j e)").broadcast_to([P, 2 * GROUP])
                             ).then_inc(rows_in[b], 16)
                sp.dma_start(id_cols[:, b, :, :],
                             group.rearrange("g j (p q) -> (g p) j q", q=TILES)
                             ).then_inc(cols_in[b], 16)

            def load_window(g, rnd, b):
                base = sp.value_load(base_row[0:1, bass.ds(g, 1)], min_val=0, max_val=max_base)
                if reaches(g, DEPTH):
                    sp.wait_ge(x_dst_summed, g - DEPTH + 1)
                if exact(g):
                    sp.dma_start(window_x[:, b, :], x[bass.ds(base, P), :]).then_inc(window_in[b], 16)
                    return
                if isinstance(g, int) and g == EXACT:
                    sp.wait_ge(x_saved, 16 * (chunks + 1))
                sp.dma_start(window[:, b, :, :].rearrange("p k f -> p (k f)"),
                             x_parts[bass.ds(base, P), :]).then_inc(window_in[b], 16)

            zero_blocks_left = []

            def fill(g, rnd, b):
                if isinstance(g, int) and g == 0 and not zero_blocks_left:
                    zero_blocks_left[:] = [(t, a) for t in range(1, TILES)
                                           for a in range(zero_blocks)]
                if isinstance(g, int) and zero_blocks_left:
                    t, a = zero_blocks_left.pop(0)
                    sp.dma_start(zero_block(t, a), zeros[:, :]).then_inc(table_set[t], 16)

            sp.wait_ge(base_row_ready, 1)
            by_flag(sp,
                    lambda: for_groups(sp, [(0, load_edges), (0, fill), (0, load_ids), (0, fill),
                                            (0, load_window), (0, fill)]),
                    lambda: for_groups(sp, [(0, load_edges), (0, fill), (0, load_ids), (0, fill),
                                            (0, fill)]))

            for q in range(TILES):
                sp.wait_ge(added[q], 16 * added_before(q, groups))
            for c in range(ln_chunks + 1):
                if c >= FIN:
                    sp.wait_ge(out_saved[c % FIN], 16 * (c // FIN))
                for q in range(TILES):
                    view, n, r = node_views(tables[q], c, ln_rows)
                    sp.dma_start(part_sb[0:n, c % FIN, q, 0:r * feat], view
                                 ).then_inc(part_in[c % FIN], 16)
            for f in range(FIN):
                sp.wait_ge(out_saved[f], 16 * ((ln_chunks + FIN - f) // FIN))

        @block.gpsimd
        def _(pool):
            pool.memset(ident[:, :], 0.0).then_inc(pool_const, 1)
            pool.memset(lower[:, :], 1.0).then_inc(pool_const, 1)
            pool.iota(lane[:, :], pattern=[[0, 1]], base=0, channel_multiplier=1,
                      allow_small_or_imprecise_dtypes=True).then_inc(pool_const, 1)
            pool.wait_ge(pool_const, 3)
            pool.affine_select(out=ident[:, :], in_=ident[:, :], compare_op=ALU.not_equal, fill=1.0,
                               base=0, pattern=[[-1, P]], channel_multiplier=1).then_inc(pool_const, 1)
            pool.affine_select(out=lower[:, :], in_=lower[:, :], compare_op=ALU.is_ge, fill=0.0,
                               base=0, pattern=[[-1, P]], channel_multiplier=1).then_inc(pool_const, 1)
            for c in range(chunks + 1):
                pool.wait_ge(x_mid, c + 1)
                pool.tensor_tensor(part_rows(c, 2), x_rows(c), part_rows(c, 1), ALU.subtract
                                   ).then_inc(x_split_ready, 1)

            def add_rows(g, rnd, b):
                pool.wait_ge(summed_ready, g + 1)
                pool.wait_ge(row_idx_ready, g + 1)
                for q in range(TILES):
                    early = isinstance(g, int) and g < EARLY
                    t = q % 2 if early else q
                    before = added_before(t, g) + (1 if early and q >= 2 else 0)
                    if isinstance(before, int) and before == 0:
                        pool.wait_ge(table_set[t], table_set_by[t])
                    else:
                        pool.wait_ge(added[t], 16 * before)
                    if reaches(g, 1):
                        pool.sem_inc(table_free, 1)
                    pool.indirect_dma_start(
                        out=tables[t],
                        out_offset=bass.IndirectOffsetOnAxis(ap=row_idx[:, b, q:q + 1], axis=0),
                        in_=summed[:, b, q * feat:(q + 1) * feat], in_offset=None,
                        compute_op=ALU.add).then_inc(added[t], 16)

            def gather_x(g, rnd, b):
                pool.wait_ge(onehot_ready, g + 1)
                if reaches(g, DEPTH):
                    pool.wait_ge(msg_ready, g - DEPTH + 1)
                pool.sem_inc(gathers_started, 1)
                for q in range(TILES):
                    pool.indirect_dma_start(
                        out=x_dst[:, b, q * feat:(q + 1) * feat], out_offset=None, in_=x,
                        in_offset=bass.IndirectOffsetOnAxis(ap=dst_idx[:, b, q:q + 1], axis=0)
                    ).then_inc(gathered[b], 16)

            by_flag(pool,
                    lambda: for_groups(pool, [(0, add_rows)]),
                    lambda: for_groups(pool, [(0, gather_x), (2, add_rows)]))

            for c in range(ln_chunks + 1):
                n, r = ln_size(c)
                zero, two, three = (part_sb[0:n, c % FIN, q, 0:r * feat] for q in (0, 2, 3))
                pool.wait_ge(part_in[c % FIN], 16 * TILES * (c // FIN + 1))
                pool.tensor_tensor(two, two, three, ALU.add).then_inc(pair23, 1)
                pool.wait_ge(pair23, c + 1)
                pool.wait_ge(pair01, c + 1)
                pool.tensor_tensor(zero, zero, two, ALU.add).then_inc(y_ready, 1)

        @block.scalar
        def _(act):
            for k in range(3):
                act.wait_ge(ids_in[k], 64 if k == 1 else 32)
                nc.scalar.activation(id_out[k][:, :, :], id_in[k][:, :, :], ACT.Copy
                                     ).then_inc(ids_ready, 1)
            for c in range(chunks + 1):
                view, n, r = node_views(x, c)
                act.dma_start(x_sb[0:n, c, 0:r * feat], view).then_inc(x_in[c], 16)
            for c in range(chunks + 2):
                if c <= chunks:
                    act.wait_ge(x_in[c], 16)
                    nc.scalar.activation(part_rows(c, 0), x_rows(c), ACT.Copy).then_inc(x_hi, 1)
                if c >= 1:
                    act.wait_ge(x_rest, c)
                    nc.scalar.activation(part_rows(c - 1, 1), x_rows(c - 1), ACT.Copy
                                         ).then_inc(x_mid, 1)
            act.wait_ge(dve_const, 5)
            nc.scalar.preload_act_table_set("natural_log_exp_and_others")

            def save_x_parts(g, rnd, b):
                if not isinstance(g, int) or g > chunks:
                    return
                act.wait_ge(x_split_ready, g + 1)
                if g == chunks:
                    view, n, r = x_parts[P * node_rows:nodes, :], tail, 1
                else:
                    main = x_parts[0:P * node_rows, :].rearrange("(p r) f -> p r f", r=node_rows)
                    view = main[:, g * x_chunk:(g + 1) * x_chunk, :].rearrange("p r f -> p (r f)")
                    n, r = P, x_chunk
                act.dma_start(view, x_split[0:n, g * x_chunk:g * x_chunk + r, :, :]
                              .rearrange("p r k f -> p (r k f)")).then_inc(x_saved, 16)

            def copy_edge_t(g, rnd, b):
                act.wait_ge(transposed, g + 1)
                if reaches(g, 2):
                    act.wait_ge(h_ready, g - 1)
                nc.scalar.activation(edge_t[:, b % 2, :], ps_t[b % 2][:, :], ACT.Copy
                                     ).then_inc(edge_t_ready, 1)

            def copy_summed(g, rnd, b):
                act.wait_ge(comb_ready, g + 1)
                if reaches(g, DEPTH):
                    act.wait_ge(table_free, TILES * (g - DEPTH + 1))
                nc.scalar.activation(summed[:, b, :], ps_c[:, :], ACT.Copy).then_inc(summed_ready, 1)

            def exp_log(g, rnd, b):
                act.wait_ge(clamped_ready, g + 1)
                nc.scalar.activation(clamped[:, b % 2, :], clamped[:, b % 2, :], ACT.Exp
                                     ).then_inc(exp_done, 1)
                act.wait_ge(exp_done, g + 1)
                nc.scalar.activation(clamped[:, b % 2, :], clamped[:, b % 2, :], ACT.Ln,
                                     bias=half[:, 0:1], scale=0.5).then_inc(log_ready, 1)

            def copy_x_dst(g, rnd, b):
                act.wait_ge(x_dst_summed, g + 1)
                if reaches(g, DEPTH):
                    act.wait_ge(msg_ready, g - DEPTH + 1)
                nc.scalar.activation(x_dst[:, b, :], ps_x[:, :], ACT.Copy).then_inc(x_dst_ready, 1)

            by_flag(act,
                    lambda: for_groups(act, [(0, copy_edge_t), (1, exp_log), (2, copy_x_dst),
                                             (3, copy_summed), (SAVE_STEP, save_x_parts)]),
                    lambda: for_groups(act, [(0, copy_edge_t), (1, exp_log), (3, copy_summed)]))

            for c in range(ln_chunks + 2):
                if c <= ln_chunks:
                    n, r = ln_size(c)
                    act.wait_ge(mean_var_ready, c + 1)
                    nc.scalar.activation(std[0:n, c % FIN, 0:r], mean_var[0:n, c % FIN, 0:r, 1],
                                         ACT.Sqrt, bias=eps[0:n, 0:1]).then_inc(std_ready, 1)
                if c >= 1:
                    act.wait_ge(norm_ready, c)
                    view, n, r = node_views(out, c - 1, ln_rows)
                    act.dma_start(view, part_sb[0:n, (c - 1) % FIN, 0, 0:r * feat]
                                  ).then_inc(out_saved[(c - 1) % FIN], 16)

        @block.vector
        def _(dve):
            done = [0]

            def then(ins):
                done[0] += 1
                ins.then_inc(prep, 1)
                dve.wait_ge(prep, done[0])

            nc.vector.memset(ones[:, :], 1.0).then_inc(dve_const, 1)
            nc.vector.memset(ones_f[:, :], 1.0).then_inc(dve_const, 1)
            nc.vector.memset(half[:, :], 0.5).then_inc(dve_const, 1)
            nc.vector.memset(eps[:, :], EPS).then_inc(dve_const, 1)
            nc.vector.memset(zeros[:, :], 0.0).then_inc(dve_const, 1)
            then(nc.vector.memset(lo[:, :], 0.0))
            then(nc.vector.memset(hi[:, :], 0.0))
            then(nc.vector.memset(base_diag[:, :], 0.0))
            for k, n in enumerate((P, second, 1)):
                dve.wait_ge(ids_in[k], 64 if k == 1 else 32)
                then(nc.vector.tensor_reduce(lo[0:n, k:k + 1], id_in[k][:, 0, :], AX.X, ALU.min))
                then(nc.vector.tensor_reduce(hi[0:n, k:k + 1], id_in[k][:, 0, :], AX.X, ALU.max))
            then(nc.vector.tensor_scalar(base_f[:, :], lo[:, :], float(max_base), None, ALU.min))
            then(nc.vector.tensor_tensor(span[:, :], hi[:, :], base_f[:, :], ALU.subtract))
            then(nc.vector.tensor_scalar(outside[:, :], span[:, :], float(P - 1), None, ALU.is_gt))
            nc.vector.tensor_reduce(outside_any[:, :], outside[:, :], AX.X, ALU.max
                                    ).then_inc(outside_ready, 1)
            dve.wait_ge(pool_const, 5)
            for k, (g0, n) in enumerate(((0, P), (P, second), (whole, 1))):
                nc.vector.tensor_scalar(base_diag[0:n, g0:g0 + n], ident[0:n, 0:n],
                                        base_f[0:n, k:k + 1], None, ALU.mult).then_inc(diag_ready, 1)
            dve.wait_ge(flag_sum, 1)
            nc.vector.tensor_scalar(flag[:, :], ps_c[0:1, 0:1], 1.0, None, ALU.min
                                    ).then_inc(flag_ready, 1)
            dve.wait_ge(base_sum, 1)
            nc.vector.tensor_copy(base_row[:, :], ps_x[0:1, 0:groups]).then_inc(base_row_ready, 1)
            then(nc.vector.tensor_scalar(window_node[:, :], ps_x[:, 0:groups], lane[:, 0:1], None,
                                         ALU.add))
            dve.wait_ge(ids_ready, 3)
            nc.vector.memset(id_out[2][:, 1, 0:repeated], trash_repeated).then_inc(repeated_set, 1)
            for c in range(chunks + 1):
                dve.wait_ge(x_hi, c + 1)
                nc.vector.tensor_tensor(x_rows(c), x_rows(c), part_rows(c, 0), ALU.subtract
                                        ).then_inc(x_rest, 1)
            dve.wait_ge(weights_in, 64)
            then(nc.vector.tensor_scalar(trash_col[:, :], lane[:, :], float(trash), None, ALU.add))
            then(nc.vector.tensor_scalar(b1_shifted[:, :], b1_col[:, :], -LN2, None, ALU.add))
            rest = b2_bc[:, :]
            for k in range(SPLITS):
                then(nc.vector.tensor_copy(b2_part[:, k, :], rest))
                then(nc.vector.tensor_tensor(b2_rest[:, k, :], rest, b2_part[:, k, :], ALU.subtract))
                rest = b2_rest[:, k, :]
            then(nc.vector.tensor_scalar(b2_sum[:, 0, :], b2_part[:, 0, :], ident[:, 0:1], None,
                                         ALU.mult))
            then(nc.vector.scalar_tensor_tensor(b2_sum[:, 1, :], b2_part[:, 1, :], ident[:, 1:2],
                                                b2_sum[:, 0, :], ALU.mult, ALU.add))
            for q in range(TILES):
                nc.vector.scalar_tensor_tensor(b2_rows[:, q, :], b2_part[:, 2, :],
                                               ident[:, 2:3], b2_sum[:, 1, :],
                                               ALU.mult, ALU.add).then_inc(b2_ready, 1)

            def clamp(g, rnd, b):
                dve.wait_ge(h_ready, g + 1)
                if reaches(g, 2):
                    dve.wait_ge(soft_ready, g - 1)
                nc.vector.tensor_scalar(clamped[:, b % 2, :], ps_h[b % 2][:, :], b1_col[:, 0:1],
                                        CLAMP, ALU.add, ALU.min).then_inc(clamped_ready, 1)

            def make_onehot(g, rnd, b):
                dve.wait_ge(rows_in[b], 16 * (rnd + 1))
                if reaches(g, 2):
                    dve.wait_ge(x_dst_summed, g - 1)
                if exact(g):
                    nc.vector.tensor_scalar(onehot_f[:, b % 2, :], id_rows[:, b, 0, :],
                                            window_node[:, g:g + 1], None, ALU.is_equal
                                            ).then_inc(onehot_ready, 1)
                    return
                nc.vector.tensor_scalar(onehot[:, b % 2, :], id_rows[:, b, 0, :],
                                        window_node[:, bass.ds(g, 1)], None, ALU.is_equal
                                        ).then_inc(onehot_ready, 1)

            def make_dst_idx(g, rnd, b):
                dve.wait_ge(cols_in[b], 16 * (rnd + 1))
                if reaches(g, DEPTH):
                    dve.wait_ge(gathered[b], 16 * TILES * rnd)
                nc.vector.tensor_copy(dst_idx[:, b, :], id_cols[:, b, 0, :]).then_inc(onehot_ready, 1)

            def make_same(g, rnd, b):
                dve.wait_ge(cols_in[b], 16 * (rnd + 1))
                nc.vector.tensor_copy(src_f[:, b, :], id_cols[:, b, 1, :]).then_inc(src_f_ready, 1)
                dve.wait_ge(rows_in[b], 16 * (rnd + 1))
                if reaches(g, 2):
                    dve.wait_ge(comb_ready, g - 1)
                dve.wait_ge(src_f_ready, g + 1)
                for q in range(TILES):
                    nc.vector.scalar_tensor_tensor(
                        same[:, b % 2, q, :], id_rows[:, b, 1, q::TILES], src_f[:, b, q:q + 1],
                        lower[:, :], ALU.is_equal, ALU.mult,
                        accum_out=n_same[:, b, q:q + 1]).then_inc(same_ready, 1)
                dve.wait_ge(same_ready, TILES * (g + 1))
                nc.vector.tensor_scalar(to_trash[:, b, :], n_same[:, b, :], 1.5, trash_col[:, 0:1],
                                        ALU.is_gt, ALU.mult).then_inc(to_trash_ready, 1)
                if reaches(g, DEPTH):
                    dve.wait_ge(table_free, TILES * (g - DEPTH + 1))
                dve.wait_ge(to_trash_ready, g + 1)
                nc.vector.tensor_tensor(row_idx[:, b, :], to_trash[:, b, :], src_f[:, b, :], ALU.max
                                        ).then_inc(row_idx_ready, 1)

            def softplus(g, rnd, b):
                dve.wait_ge(log_ready, g + 1)
                nc.vector.scalar_tensor_tensor(soft[:, b % 2, :], ps_h[b % 2][:, :],
                                               b1_shifted[:, 0:1], clamped[:, b % 2, :],
                                               ALU.add, ALU.max).then_inc(soft_ready, 1)

            def multiply(g, rnd, b):
                dve.wait_ge(w_ready, g + 1)
                nc.vector.tensor_tensor(msg[:, b % 2, :], ps_w[b % 2][:, :], x_dst[:, b, :], ALU.mult
                                        ).then_inc(msg_ready, 1)

            def multiply_summed(g, rnd, b):
                dve.wait_ge(x_dst_ready, g + 1)
                multiply(g, rnd, b)

            def multiply_gathered(g, rnd, b):
                dve.wait_ge(gathered[b], 16 * TILES * (rnd + 1))
                multiply(g, rnd, b)

            by_flag(dve,
                    lambda: for_groups(dve, [(3, multiply_summed), (1, clamp), (2, make_same),
                                             (1, make_onehot), (1, softplus)]),
                    lambda: for_groups(dve, [(3, multiply_gathered), (1, clamp), (2, make_same),
                                             (1, make_dst_idx), (1, softplus)]))

            def add_01(c):
                n, r = ln_size(c)
                zero, one = (part_sb[0:n, c % FIN, q, 0:r * feat] for q in range(2))
                dve.wait_ge(part_in[c % FIN], 16 * TILES * (c // FIN + 1))
                nc.vector.tensor_tensor(zero, zero, one, ALU.add).then_inc(pair01, 1)

            def statistics(c):
                n, r = ln_size(c)
                f = c % FIN
                dve.wait_ge(y_ready, c + 1)
                for k in range(r):
                    last = nc.vector.bn_stats(stats[0:n, f, k, :],
                                              part_sb[0:n, f, 0, k * feat:(k + 1) * feat])
                last.then_inc(stats_ready, 1)
                dve.wait_ge(stats_ready, c + 1)
                for k in range(r):
                    last = nc.vector.bn_aggr(mean_var[0:n, f, k, :], stats[0:n, f, k, :])
                last.then_inc(mean_var_ready, 1)

            def normalise(c):
                n, r = ln_size(c)
                f = c % FIN
                dve.wait_ge(std_ready, c + 1)
                nc.vector.reciprocal(rstd[0:n, f, 0:r], std[0:n, f, 0:r]).then_inc(rstd_ready, 1)
                dve.wait_ge(rstd_ready, c + 1)
                for k in range(r):
                    row = part_sb[0:n, f, 0, k * feat:(k + 1) * feat]
                    last = nc.vector.tensor_scalar(row, row, mean_var[0:n, f, k, 0:1],
                                                   rstd[0:n, f, k:k + 1], ALU.subtract, ALU.mult)
                last.then_inc(norm_ready, 1)

            for step in range(ln_chunks + 3):
                for late, part in ((0, add_01), (2, normalise), (1, statistics)):
                    if 0 <= step - late <= ln_chunks:
                        part(step - late)

        @block.tensor
        def _(pe):
            pe.wait_ge(dve_const, 5)
            pe.wait_ge(outside_ready, 1)
            nc.tensor.matmul(ps_c[0:1, 0:1], outside_any[:, :], ones_f[:, 0:1], start=True, stop=True
                             ).then_inc(flag_sum, 1)
            pe.wait_ge(diag_ready, 3)
            nc.tensor.matmul(ps_x[:, 0:groups], ones_f[:, :], base_diag[:, :], start=True, stop=True
                             ).then_inc(base_sum, 1)
            pe.wait_ge(weights_in, 64)
            pe.wait_ge(pool_const, 5)

            def transpose(g, rnd, b):
                pe.wait_ge(edge_in[b], 16 * (rnd + 1))
                if reaches(g, 2):
                    pe.wait_ge(edge_t_ready, g - 1)
                for q in range(TILES):
                    last = nc.tensor.transpose(ps_t[b % 2][:, q * P:(q + 1) * P],
                                               edge_sb[:, b, q, :], ident[:, :])
                last.then_inc(transposed, 1)

            def combine(g, rnd, b):
                pe.wait_ge(msg_ready, g + 1)
                pe.wait_ge(row_idx_ready, g + 1)
                if reaches(g, 1):
                    pe.wait_ge(summed_ready, g)
                for q in range(TILES):
                    last = nc.tensor.matmul(ps_c[:, q * P:(q + 1) * P], same[:, b % 2, q, :],
                                            msg[:, b % 2, q * P:(q + 1) * P], start=True, stop=True)
                last.then_inc(comb_ready, 1)

            def layer1(g, rnd, b):
                pe.wait_ge(edge_t_ready, g + 1)
                if reaches(g, 2):
                    pe.wait_ge(soft_ready, g - 1)
                nc.tensor.matmul(ps_h[b % 2][:, :], w1_sb[:, :], edge_t[:, b % 2, :],
                                 start=True, stop=True).then_inc(h_ready, 1)

            def sum_x_dst(g, rnd, b):
                pe.wait_ge(onehot_ready, g + 1)
                pe.wait_ge(window_in[b], 16 * (rnd + 1))
                if reaches(g, 1):
                    pe.wait_ge(x_dst_ready, g)
                if exact(g):
                    for q in range(TILES):
                        last = nc.tensor.matmul(ps_x[:, q * P:(q + 1) * P],
                                                onehot_f[:, b % 2, q::TILES], window_x[:, b, :],
                                                start=True, stop=True)
                    last.then_inc(x_dst_summed, 1)
                    return
                for q in range(TILES):
                    for k in range(SPLITS):
                        last = nc.tensor.matmul(ps_x[:, q * P:(q + 1) * P],
                                                onehot[:, b % 2, q::TILES], window[:, b, k, :],
                                                start=(k == 0), stop=(k == SPLITS - 1))
                last.then_inc(x_dst_summed, 1)

            def layer2(g, rnd, b):
                if reaches(g, 2):
                    pe.wait_ge(msg_ready, g - 1)
                if isinstance(g, int) and g == 0:
                    pe.wait_ge(b2_ready, TILES)
                nc.tensor.matmul(ps_w[b % 2][:, :], ones[:, :],
                                 b2_rows[:, :, :].rearrange("p q f -> p (q f)"),
                                 start=True, stop=False, skip_group_check=True)
                pe.wait_ge(soft_ready, g + 1)
                for q in range(TILES):
                    last = nc.tensor.matmul(ps_w[b % 2][:, q * P:(q + 1) * P],
                                            soft[:, b % 2, q * P:(q + 1) * P], w2_sb[:, :],
                                            start=False, stop=True, skip_group_check=True)
                last.then_inc(w_ready, 1)

            by_flag(pe,
                    lambda: for_groups(pe, [(0, transpose), (1, layer1), (2, sum_x_dst),
                                            (3, combine), (2, layer2)]),
                    lambda: for_groups(pe, [(0, transpose), (1, layer1), (3, combine),
                                            (2, layer2)]))


_INPUTS = ["x", "src", "dst", "edge_attr_128", "L0_gnn_W1", "L0_gnn_b1", "L0_gnn_W2", "L0_gnn_b2"]


def kernel(**inputs):
    from concourse import bacc
    from concourse.bass_utils import run_bass_kernel_spmd

    nc = bacc.Bacc("TRN2", target_bir_lowering=False, num_devices=1)
    arrays, views = {}, []
    for name in _INPUTS:
        a = np.ascontiguousarray(inputs[name])
        arrays[f"in_{name}"] = a
        views.append(nc.dram_tensor(f"in_{name}", a.shape, mybir.dt.from_np(a.dtype),
                                    kind="ExternalInput").ap())
    shape = np.asarray(inputs["x"]).shape
    views.append(nc.dram_tensor("out", shape, mybir.dt.float32, kind="ExternalOutput").ap())
    gnn_program(nc, *views)
    return run_bass_kernel_spmd(nc, [arrays], core_ids=[0]).results[0]["out"]
```

```python
import math
from contextlib import ExitStack

import numpy as np

import concourse.bass as bass
from concourse import mybir

P = 128
TILES = 4
GROUP = P * TILES
DEPTH = 4
LN2 = math.log(2.0)
EPS = 1e-5
SPLITS = 3
PEELED = 3
TWO_TABLES = 1
THREE_TABLES = 2
FILLS = (1, 1, 1, 3, 5, 2, 2, 2, 2, 1)
CLAMP = 20.0


def gnn_program(nc, x, src, dst, edge, w1, b1, w2, b2, out):
    fp32, bf16 = mybir.dt.float32, mybir.dt.bfloat16
    i32, u16 = mybir.dt.int32, mybir.dt.uint16
    ALU, ACT, AX = mybir.AluOpType, mybir.ActivationFunctionType, mybir.AxisListType

    nodes, feat = x.shape
    edges = edge.shape[0]
    assert feat == P
    groups = -(-edges // GROUP)
    whole = edges // GROUP
    assert groups == whole + 1 and groups % DEPTH == 0
    last_start = edges - GROUP
    repeated = whole * GROUP - last_start
    trash_repeated = nodes
    trash = nodes + 1
    table_rows = -(-(nodes + P + 1) // P) * P
    zero_rows = 10
    assert table_rows % (P * zero_rows) == 0
    max_base = nodes - P

    node_rows = nodes // P
    tail = nodes - P * node_rows

    second = whole - P

    ctx = ExitStack()
    with ctx:
        def sb(name, shape, dtype):
            return ctx.enter_context(nc.sbuf_tensor(name, shape, dtype))

        def bank(name):
            return ctx.enter_context(nc.psum_tensor(name, [P, GROUP], fp32))

        def sem(name):
            return ctx.enter_context(nc.semaphore(name))

        def sems(name, n):
            return [sem(f"{name}{k}") for k in range(n)]

        tables = [nc.dram_tensor(f"table{q}", (table_rows, feat), fp32, kind="Internal").ap()
                  for q in range(TILES)]
        ids = nc.dram_tensor("ids", (groups, 2, GROUP), u16, kind="Internal").ap()

        ident = sb("ident", [P, P], fp32)
        lower = sb("lower", [P, P], fp32)
        ones = sb("ones", [P, P], bf16)
        half = sb("half", [P, 1], fp32)
        eps = sb("eps", [P, 1], fp32)
        lane = sb("lane", [P, 1], fp32)
        trash_col = sb("trash_col", [P, 1], fp32)
        zeros = sb("zeros", [P, zero_rows * feat], fp32)
        ones_f = sb("ones_f", [P, P], fp32)
        w1_sb = sb("w1_sb", [P, P], fp32)
        w2_sb = sb("w2_sb", [P, P], fp32)
        b1_col = sb("b1_col", [P, 1], fp32)
        b1_shifted = sb("b1_shifted", [P, 1], fp32)
        b2_bc = sb("b2_bc", [P, P], fp32)
        b2_part = sb("b2_part", [P, SPLITS, P], bf16)
        b2_rest = sb("b2_rest", [P, SPLITS, P], fp32)
        b2_sum = sb("b2_sum", [P, 2, P], bf16)
        b2_rows = sb("b2_rows", [P, TILES, P], bf16)

        id_in = [sb(f"id_in{k}", [n, 2, GROUP], i32) for k, n in enumerate((P, second, 1))]
        id_out = [sb(f"id_out{k}", [n, 2, GROUP], u16) for k, n in enumerate((P, second, 1))]
        lo = sb("lo", [P, 3], fp32)
        hi = sb("hi", [P, 3], fp32)
        base_f = sb("base_f", [P, 3], fp32)
        base_diag = sb("base_diag", [P, groups], fp32)
        span = sb("span", [P, 3], fp32)
        outside = sb("outside", [P, 3], fp32)
        outside_any = sb("outside_any", [P, 1], fp32)
        flag = sb("flag", [1, 1], i32)
        base_row = sb("base_row", [1, groups], i32)
        window_node = sb("window_node", [P, groups], fp32)

        edge_sb = sb("edge_sb", [P, DEPTH, TILES, feat], fp32)
        edge_t = sb("edge_t", [P, 2, GROUP], fp32)
        id_rows = sb("id_rows", [P, DEPTH, 2, GROUP], u16)
        id_cols = sb("id_cols", [P, DEPTH, 2, TILES], u16)
        window = sb("window", [P, DEPTH, SPLITS, feat], bf16)
        window_x = sb("window_x", [P, DEPTH, feat], fp32)
        onehot = sb("onehot", [P, 2, GROUP], bf16)
        dst_idx = sb("dst_idx", [P, DEPTH, TILES], i32)
        src_f = sb("src_f", [P, DEPTH, TILES], fp32)
        same = sb("same", [P, 2, TILES, P], fp32)
        n_same = sb("n_same", [P, DEPTH, TILES], fp32)
        to_trash = sb("to_trash", [P, DEPTH, TILES], fp32)
        row_idx = sb("row_idx", [P, DEPTH, TILES], i32)
        clamped = sb("clamped", [P, 2, GROUP], fp32)
        soft = sb("soft", [P, 2, GROUP], fp32)
        x_dst = sb("x_dst", [P, DEPTH, GROUP], fp32)
        msg = sb("msg", [P, 2, GROUP], fp32)
        summed = sb("summed", [P, DEPTH, GROUP], fp32)

        FIN = 8
        ln_rows = 4
        ln_chunks = node_rows // ln_rows
        assert ln_chunks * ln_rows == node_rows
        part_sb = sb("part_sb", [P, FIN, TILES, ln_rows * feat], fp32)
        stats = sb("stats", [P, FIN, ln_rows, 6], fp32)
        mean_var = sb("mean_var", [P, FIN, ln_rows, 2], fp32)
        std = sb("std", [P, FIN, ln_rows], fp32)
        rstd = sb("rstd", [P, FIN, ln_rows], fp32)

        ps_t = [bank(f"ps_t{k}") for k in range(2)]
        ps_h = [bank(f"ps_h{k}") for k in range(2)]
        ps_w = [bank(f"ps_w{k}") for k in range(2)]
        ps_x = bank("ps_x")
        ps_c = bank("ps_c")

        weights_in = sem("weights_in")
        ids_in = sems("ids_in", 3)
        pool_const = sem("pool_const")
        dve_const = sem("dve_const")
        prep = sem("prep")
        ids_ready = sem("ids_ready")
        repeated_set = sem("repeated_set")
        ids_saved = sem("ids_saved")
        outside_ready = sem("outside_ready")
        flag_sum = sem("flag_sum")
        flag_ready = sem("flag_ready")
        diag_ready = sem("diag_ready")
        base_sum = sem("base_sum")
        base_row_ready = sem("base_row_ready")
        b2_ready = sem("b2_ready")
        table_set = sems("table_set", TILES)
        edge_in = sems("edge_in", DEPTH)
        rows_in = sems("rows_in", DEPTH)
        cols_in = sems("cols_in", DEPTH)
        window_in = sems("window_in", DEPTH)
        gathered = sems("gathered", DEPTH)
        added = sems("added", TILES)
        transposed = sem("transposed")
        edge_t_ready = sem("edge_t_ready")
        h_ready = sem("h_ready")
        clamped_ready = sem("clamped_ready")
        exp_done = sem("exp_done")
        log_ready = sem("log_ready")
        soft_ready = sem("soft_ready")
        onehot_ready = sem("onehot_ready")
        x_hi = sem("x_hi")
        x_rest = sem("x_rest")
        x_mid = sem("x_mid")
        x_low = sem("x_low")
        x_dst_summed = sem("x_dst_summed")
        x_dst_ready = sem("x_dst_ready")
        w_ready = sem("w_ready")
        msg_ready = sem("msg_ready")
        src_f_ready = sem("src_f_ready")
        same_ready = sem("same_ready")
        to_trash_ready = sem("to_trash_ready")
        row_idx_ready = sem("row_idx_ready")
        comb_ready = sem("comb_ready")
        summed_ready = sem("summed_ready")
        gathers_started = sem("gathers_started")
        table_free = sem("table_free")
        part_in = sems("part_in", FIN)
        pair01 = sem("pair01")
        pair23 = sem("pair23")
        y_ready = sem("y_ready")
        stats_ready = sem("stats_ready")
        mean_var_ready = sem("mean_var_ready")
        std_ready = sem("std_ready")
        rstd_ready = sem("rstd_ready")
        norm_ready = sem("norm_ready")
        out_saved = sems("out_saved", FIN)

        block = ctx.enter_context(nc.Block())

        def at(rnd, off):
            return rnd * DEPTH + off, rnd + off // DEPTH, off % DEPTH

        def for_groups(eng, stages):
            late = max(k for k, _ in stages)
            first, end = PEELED, groups // DEPTH - 1

            def peeled(s):
                for k, stage in stages:
                    if 0 <= s - k < groups:
                        stage(s - k, (s - k) // DEPTH, (s - k) % DEPTH)

            for s in range(first * DEPTH):
                peeled(s)
            with eng.Fori(first, end) as rnd:
                for u in range(DEPTH):
                    for k, stage in stages:
                        stage(*at(rnd, u - k))
            for s in range(end * DEPTH, groups + late):
                peeled(s)

        def reaches(g, n):
            return not isinstance(g, int) or g >= n

        def table_of(g, q):
            if isinstance(g, int) and g < TWO_TABLES:
                return q % 2
            if isinstance(g, int) and g < THREE_TABLES:
                return (TILES * g + q) % 3
            return q

        def added_before(t, g, q=0):
            if isinstance(g, int):
                return sum(table_of(h, k) == t for h in range(g + 1)
                           for k in range(q if h == g else TILES))
            return g + (added_before(t, THREE_TABLES) - THREE_TABLES)

        def by_flag(eng, sorted_path, general_path):
            eng.wait_ge(flag_ready, 1)
            value = eng.value_load(flag[0:1, 0:1], min_val=0, max_val=1)
            with eng.If(value == 0):
                sorted_path()
            with eng.Else():
                general_path()

        def node_views(dram, c, rows):
            if c == node_rows // rows:
                return dram[P * node_rows:nodes, :], tail, 1
            main = dram[0:P * node_rows, :].rearrange("(p r) f -> p r f", r=node_rows)
            return (main[:, c * rows:(c + 1) * rows, :].rearrange("p r f -> p (r f)"), P, rows)

        def ln_size(c):
            return (tail, 1) if c == ln_chunks else (P, ln_rows)

        def zero_block(t, a):
            return tables[t].rearrange("(p a r) f -> a p (r f)", p=P, r=zero_rows)[a]

        zero_blocks = table_rows // (P * zero_rows)
        x_pieces = 3
        assert node_rows % x_pieces == 0
        table_set_by = [16 * (x_pieces + 2)] + [16 * zero_blocks] * (TILES - 1)

        @block.sync
        def _(sp):
            for k, g0, n in ((0, 0, P), (1, P, second), (2, None, 1)):
                for j, a in ((0, dst), (1, src)):
                    e0 = last_start if k == 2 else g0 * GROUP
                    view = a[e0:e0 + n * GROUP].rearrange("(p e) -> p e", p=n)
                    sp.dma_start(id_in[k][:, j, :], view).then_inc(ids_in[k], 16)

            sp.dma_start(w1_sb[:, :], w1).then_inc(weights_in, 16)
            sp.dma_start(w2_sb[:, :], w2).then_inc(weights_in, 16)
            sp.dma_start(b1_col[:, :], b1.rearrange("(p o) -> p o", o=1)).then_inc(weights_in, 16)
            sp.dma_start(b2_bc[:, :], b2.rearrange("(o f) -> o f", o=1).broadcast_to([P, feat])
                         ).then_inc(weights_in, 16)

            def start_of(g):
                return last_start if isinstance(g, int) and g == whole else g * GROUP

            def load_edges(g, rnd, b):
                if reaches(g, DEPTH):
                    sp.wait_ge(transposed, g - DEPTH + 1)
                sp.dma_start(edge_sb[:, b, :, :].rearrange("p q f -> p (q f)"),
                             edge[bass.ds(start_of(g), GROUP), :]
                             .rearrange("(p q) f -> p (q f)", q=TILES)).then_inc(edge_in[b], 16)

            def set_x(r0, r1):
                rows = [a[0:P * node_rows, :].rearrange("(p r) f -> p r f", r=node_rows)
                        [:, r0:r1, :].rearrange("p r f -> p (r f)") for a in (tables[0], x)]
                sp.dma_start(*rows).then_inc(table_set[0], 16)

            piece = node_rows // x_pieces
            for g in range(DEPTH):
                load_edges(g, 0, g)
            sp.wait_ge(ids_saved, 16 * 3)

            def load_next_edges(g, rnd, b):
                if reaches(g, DEPTH):
                    load_edges(g, rnd, b)

            def load_ids(g, rnd, b):
                if reaches(g, DEPTH):
                    sp.wait_ge(onehot_ready, g - DEPTH + 1)
                    sp.wait_ge(row_idx_ready, g - DEPTH + 1)
                group = ids[bass.ds(g, 1), :, :]
                sp.dma_start(id_rows[:, b, :, :].rearrange("p j e -> p (j e)"),
                             group.rearrange("g j e -> g (j e)").broadcast_to([P, 2 * GROUP])
                             ).then_inc(rows_in[b], 16)
                sp.dma_start(id_cols[:, b, :, :],
                             group.rearrange("g j (p q) -> (g p) j q", q=TILES)
                             ).then_inc(cols_in[b], 16)

            def load_window(g, rnd, b):
                base = sp.value_load(base_row[0:1, bass.ds(g, 1)], min_val=0, max_val=max_base)
                if reaches(g, DEPTH):
                    sp.wait_ge(x_low, g - DEPTH + 1)
                sp.dma_start(window_x[:, b, :], x[bass.ds(base, P), :]).then_inc(window_in[b], 16)

            def set_part(n):
                if n < x_pieces:
                    set_x(n * piece, (n + 1) * piece)
                elif n == x_pieces:
                    sp.dma_start(tables[0][P * node_rows:nodes, :], x[P * node_rows:nodes, :]
                                 ).then_inc(table_set[0], 16)
                elif n == x_pieces + 1:
                    sp.dma_start(tables[0][nodes:table_rows, :]
                                 .rearrange("(p r) f -> p (r f)", r=2),
                                 zeros[0:(table_rows - nodes) // 2, 0:2 * feat]
                                 ).then_inc(table_set[0], 16)
                else:
                    t, a = divmod(n - x_pieces - 2, zero_blocks)
                    sp.dma_start(zero_block(t + 1, a), zeros[:, :]).then_inc(table_set[t + 1], 16)

            assert sum(FILLS) == x_pieces + 2 + (TILES - 1) * zero_blocks
            assert len(FILLS) <= PEELED * DEPTH

            def fill(g, rnd, b):
                if isinstance(g, int):
                    for n in range(sum(FILLS[0:g + 1]), sum(FILLS[0:g + 2])):
                        set_part(n)

            for n in range(FILLS[0]):
                set_part(n)
            sp.wait_ge(dve_const, 5)
            sp.wait_ge(base_row_ready, 1)
            by_flag(sp,
                    lambda: for_groups(sp, [(0, load_window), (0, load_next_edges), (0, load_ids),
                                            (0, fill)]),
                    lambda: for_groups(sp, [(0, load_next_edges), (0, load_ids), (0, fill)]))

            for q in range(TILES):
                sp.wait_ge(added[q], 16 * added_before(q, groups))
            for c in range(ln_chunks + 1):
                if c >= FIN:
                    sp.wait_ge(out_saved[c % FIN], 16 * (c // FIN))
                for q in range(TILES):
                    view, n, r = node_views(tables[q], c, ln_rows)
                    sp.dma_start(part_sb[0:n, c % FIN, q, 0:r * feat], view
                                 ).then_inc(part_in[c % FIN], 16)
            for f in range(FIN):
                sp.wait_ge(out_saved[f], 16 * ((ln_chunks + FIN - f) // FIN))

        @block.gpsimd
        def _(pool):
            pool.memset(ident[:, :], 0.0).then_inc(pool_const, 1)
            pool.memset(lower[:, :], 1.0).then_inc(pool_const, 1)
            pool.iota(lane[:, :], pattern=[[0, 1]], base=0, channel_multiplier=1,
                      allow_small_or_imprecise_dtypes=True).then_inc(pool_const, 1)
            pool.wait_ge(pool_const, 3)
            pool.affine_select(out=ident[:, :], in_=ident[:, :], compare_op=ALU.not_equal, fill=1.0,
                               base=0, pattern=[[-1, P]], channel_multiplier=1).then_inc(pool_const, 1)
            pool.affine_select(out=lower[:, :], in_=lower[:, :], compare_op=ALU.is_ge, fill=0.0,
                               base=0, pattern=[[-1, P]], channel_multiplier=1).then_inc(pool_const, 1)
            def add_rows(g, rnd, b):
                pool.wait_ge(summed_ready, g + 1)
                for q in range(TILES):
                    t = table_of(g, q)
                    before = added_before(t, g, q)
                    if isinstance(before, int) and before == 0:
                        pool.wait_ge(table_set[t], table_set_by[t])
                    else:
                        pool.wait_ge(added[t], 16 * before)
                    if reaches(g, 1):
                        pool.sem_inc(table_free, 1)
                    pool.indirect_dma_start(
                        out=tables[t],
                        out_offset=bass.IndirectOffsetOnAxis(ap=row_idx[:, b, q:q + 1], axis=0),
                        in_=summed[:, b, q * feat:(q + 1) * feat], in_offset=None,
                        compute_op=ALU.add).then_inc(added[t], 16)

            def gather_x(g, rnd, b):
                pool.wait_ge(onehot_ready, g + 1)
                if reaches(g, DEPTH):
                    pool.wait_ge(msg_ready, g - DEPTH + 1)
                pool.sem_inc(gathers_started, 1)
                for q in range(TILES):
                    pool.indirect_dma_start(
                        out=x_dst[:, b, q * feat:(q + 1) * feat], out_offset=None, in_=x,
                        in_offset=bass.IndirectOffsetOnAxis(ap=dst_idx[:, b, q:q + 1], axis=0)
                    ).then_inc(gathered[b], 16)

            by_flag(pool,
                    lambda: for_groups(pool, [(0, add_rows)]),
                    lambda: for_groups(pool, [(0, gather_x), (2, add_rows)]))

            for c in range(ln_chunks + 1):
                n, r = ln_size(c)
                zero, two, three = (part_sb[0:n, c % FIN, q, 0:r * feat] for q in (0, 2, 3))
                pool.wait_ge(part_in[c % FIN], 16 * TILES * (c // FIN + 1))
                pool.tensor_tensor(two, two, three, ALU.add).then_inc(pair23, 1)
                pool.wait_ge(pair23, c + 1)
                pool.wait_ge(pair01, c + 1)
                pool.tensor_tensor(zero, zero, two, ALU.add).then_inc(y_ready, 1)

        @block.scalar
        def _(act):
            for k in range(3):
                act.wait_ge(ids_in[k], 32)
                nc.scalar.activation(id_out[k][:, :, :], id_in[k][:, :, :], ACT.Copy
                                     ).then_inc(ids_ready, 1)
            for k, g0, n in ((0, 0, P), (1, P, second), (2, whole, 1)):
                act.wait_ge(ids_ready, k + 1)
                if k == 2:
                    act.wait_ge(repeated_set, 1)
                act.dma_start(ids[g0:g0 + n, :, :].rearrange("g j e -> g (j e)"),
                              id_out[k][:, :, :].rearrange("g j e -> g (j e)")
                              ).then_inc(ids_saved, 16)
            act.wait_ge(dve_const, 5)
            nc.scalar.preload_act_table_set("natural_log_exp_and_others")

            def split_hi(g, rnd, b):
                act.wait_ge(window_in[b], 16 * (rnd + 1))
                if reaches(g, DEPTH):
                    act.wait_ge(x_dst_summed, g - DEPTH + 1)
                nc.scalar.activation(window[:, b, 0, :], window_x[:, b, :], ACT.Copy
                                     ).then_inc(x_hi, 1)

            def split_mid(g, rnd, b):
                act.wait_ge(x_rest, g + 1)
                nc.scalar.activation(window[:, b, 1, :], window_x[:, b, :], ACT.Copy
                                     ).then_inc(x_mid, 1)

            def copy_edge_t(g, rnd, b):
                act.wait_ge(transposed, g + 1)
                if reaches(g, 2):
                    act.wait_ge(h_ready, g - 1)
                nc.scalar.activation(edge_t[:, b % 2, :], ps_t[b % 2][:, :], ACT.Copy
                                     ).then_inc(edge_t_ready, 1)

            def copy_summed(g, rnd, b):
                act.wait_ge(comb_ready, g + 1)
                if reaches(g, DEPTH):
                    act.wait_ge(table_free, TILES * (g - DEPTH + 1))
                nc.scalar.activation(summed[:, b, :], ps_c[:, :], ACT.Copy).then_inc(summed_ready, 1)

            def exp_log(g, rnd, b):
                act.wait_ge(clamped_ready, g + 1)
                nc.scalar.activation(clamped[:, b % 2, :], clamped[:, b % 2, :], ACT.Exp
                                     ).then_inc(exp_done, 1)
                act.wait_ge(exp_done, g + 1)
                nc.scalar.activation(clamped[:, b % 2, :], clamped[:, b % 2, :], ACT.Ln,
                                     bias=half[:, 0:1], scale=0.5).then_inc(log_ready, 1)

            def copy_x_dst(g, rnd, b):
                act.wait_ge(x_dst_summed, g + 1)
                if reaches(g, DEPTH):
                    act.wait_ge(msg_ready, g - DEPTH + 1)
                nc.scalar.activation(x_dst[:, b, :], ps_x[:, :], ACT.Copy).then_inc(x_dst_ready, 1)

            by_flag(act,
                    lambda: for_groups(act, [(0, split_hi), (1, split_mid), (0, copy_edge_t), (1, exp_log),
                                             (2, copy_x_dst), (3, copy_summed)]),
                    lambda: for_groups(act, [(0, copy_edge_t), (1, exp_log), (3, copy_summed)]))

            for c in range(ln_chunks + 2):
                if c <= ln_chunks:
                    n, r = ln_size(c)
                    act.wait_ge(mean_var_ready, c + 1)
                    nc.scalar.activation(std[0:n, c % FIN, 0:r], mean_var[0:n, c % FIN, 0:r, 1],
                                         ACT.Sqrt, bias=eps[0:n, 0:1]).then_inc(std_ready, 1)
                if c >= 1:
                    act.wait_ge(norm_ready, c)
                    view, n, r = node_views(out, c - 1, ln_rows)
                    act.dma_start(view, part_sb[0:n, (c - 1) % FIN, 0, 0:r * feat]
                                  ).then_inc(out_saved[(c - 1) % FIN], 16)

        @block.vector
        def _(dve):
            done = [0]

            def then(ins):
                done[0] += 1
                ins.then_inc(prep, 1)
                dve.wait_ge(prep, done[0])

            nc.vector.memset(ones[:, :], 1.0).then_inc(dve_const, 1)
            nc.vector.memset(ones_f[:, :], 1.0).then_inc(dve_const, 1)
            nc.vector.memset(half[:, :], 0.5).then_inc(dve_const, 1)
            nc.vector.memset(eps[:, :], EPS).then_inc(dve_const, 1)
            nc.vector.memset(zeros[:, :], 0.0).then_inc(dve_const, 1)
            then(nc.vector.memset(lo[:, :], 0.0))
            then(nc.vector.memset(hi[:, :], 0.0))
            then(nc.vector.memset(base_diag[:, :], 0.0))
            for k, n in enumerate((P, second, 1)):
                dve.wait_ge(ids_in[k], 32)
                then(nc.vector.tensor_reduce(lo[0:n, k:k + 1], id_in[k][:, 0, :], AX.X, ALU.min))
                then(nc.vector.tensor_reduce(hi[0:n, k:k + 1], id_in[k][:, 0, :], AX.X, ALU.max))
            dve.wait_ge(ids_ready, 3)
            nc.vector.memset(id_out[2][:, 1, 0:repeated], trash_repeated).then_inc(repeated_set, 1)
            then(nc.vector.tensor_scalar(base_f[:, :], lo[:, :], float(max_base), None, ALU.min))
            then(nc.vector.tensor_tensor(span[:, :], hi[:, :], base_f[:, :], ALU.subtract))
            then(nc.vector.tensor_scalar(outside[:, :], span[:, :], float(P - 1), None, ALU.is_gt))
            nc.vector.tensor_reduce(outside_any[:, :], outside[:, :], AX.X, ALU.max
                                    ).then_inc(outside_ready, 1)
            dve.wait_ge(pool_const, 5)
            for k, (g0, n) in enumerate(((0, P), (P, second), (whole, 1))):
                nc.vector.tensor_scalar(base_diag[0:n, g0:g0 + n], ident[0:n, 0:n],
                                        base_f[0:n, k:k + 1], None, ALU.mult).then_inc(diag_ready, 1)
            dve.wait_ge(flag_sum, 1)
            nc.vector.tensor_scalar(flag[:, :], ps_c[0:1, 0:1], 1.0, None, ALU.min
                                    ).then_inc(flag_ready, 1)
            dve.wait_ge(base_sum, 1)
            nc.vector.tensor_copy(base_row[:, :], ps_x[0:1, 0:groups]).then_inc(base_row_ready, 1)
            then(nc.vector.tensor_scalar(window_node[:, :], ps_x[:, 0:groups], lane[:, 0:1], None,
                                         ALU.add))
            dve.wait_ge(weights_in, 64)
            then(nc.vector.tensor_scalar(trash_col[:, :], lane[:, :], float(trash), None, ALU.add))
            then(nc.vector.tensor_scalar(b1_shifted[:, :], b1_col[:, :], -LN2, None, ALU.add))
            rest = b2_bc[:, :]
            for k in range(SPLITS):
                then(nc.vector.tensor_copy(b2_part[:, k, :], rest))
                then(nc.vector.tensor_tensor(b2_rest[:, k, :], rest, b2_part[:, k, :], ALU.subtract))
                rest = b2_rest[:, k, :]
            then(nc.vector.tensor_scalar(b2_sum[:, 0, :], b2_part[:, 0, :], ident[:, 0:1], None,
                                         ALU.mult))
            then(nc.vector.scalar_tensor_tensor(b2_sum[:, 1, :], b2_part[:, 1, :], ident[:, 1:2],
                                                b2_sum[:, 0, :], ALU.mult, ALU.add))
            for q in range(TILES):
                nc.vector.scalar_tensor_tensor(b2_rows[:, q, :], b2_part[:, 2, :],
                                               ident[:, 2:3], b2_sum[:, 1, :],
                                               ALU.mult, ALU.add).then_inc(b2_ready, 1)

            def clamp(g, rnd, b):
                dve.wait_ge(h_ready, g + 1)
                if reaches(g, 2):
                    dve.wait_ge(soft_ready, g - 1)
                nc.vector.tensor_scalar(clamped[:, b % 2, :], ps_h[b % 2][:, :], b1_col[:, 0:1],
                                        CLAMP, ALU.add, ALU.min).then_inc(clamped_ready, 1)

            def make_onehot(g, rnd, b):
                dve.wait_ge(rows_in[b], 16 * (rnd + 1))
                if reaches(g, 2):
                    dve.wait_ge(x_dst_summed, g - 1)
                nc.vector.tensor_scalar(onehot[:, b % 2, :], id_rows[:, b, 0, :],
                                        window_node[:, bass.ds(g, 1)], None, ALU.is_equal
                                        ).then_inc(onehot_ready, 1)

            def split_rest(g, rnd, b):
                dve.wait_ge(x_hi, g + 1)
                nc.vector.tensor_tensor(window_x[:, b, :], window_x[:, b, :], window[:, b, 0, :],
                                        ALU.subtract).then_inc(x_rest, 1)

            def split_low(g, rnd, b):
                dve.wait_ge(x_mid, g + 1)
                nc.vector.tensor_tensor(window[:, b, 2, :], window_x[:, b, :], window[:, b, 1, :],
                                        ALU.subtract).then_inc(x_low, 1)

            def make_dst_idx(g, rnd, b):
                dve.wait_ge(cols_in[b], 16 * (rnd + 1))
                if reaches(g, DEPTH):
                    dve.wait_ge(gathered[b], 16 * TILES * rnd)
                nc.vector.tensor_copy(dst_idx[:, b, :], id_cols[:, b, 0, :]).then_inc(onehot_ready, 1)

            def copy_src(g, rnd, b):
                dve.wait_ge(cols_in[b], 16 * (rnd + 1))
                nc.vector.tensor_copy(src_f[:, b, :], id_cols[:, b, 1, :]).then_inc(src_f_ready, 1)

            def make_same(g, rnd, b):
                dve.wait_ge(rows_in[b], 16 * (rnd + 1))
                if reaches(g, 2):
                    dve.wait_ge(comb_ready, g - 1)
                dve.wait_ge(src_f_ready, g + 1)
                for q in range(TILES):
                    nc.vector.scalar_tensor_tensor(
                        same[:, b % 2, q, :], id_rows[:, b, 1, q::TILES], src_f[:, b, q:q + 1],
                        lower[:, :], ALU.is_equal, ALU.mult,
                        accum_out=n_same[:, b, q:q + 1]).then_inc(same_ready, 1)

            def find_trash(g, rnd, b):
                dve.wait_ge(same_ready, TILES * (g + 1))
                nc.vector.tensor_scalar(to_trash[:, b, :], n_same[:, b, :], 1.5, trash_col[:, 0:1],
                                        ALU.is_gt, ALU.mult).then_inc(to_trash_ready, 1)

            def make_row_idx(g, rnd, b):
                if reaches(g, DEPTH):
                    dve.wait_ge(table_free, TILES * (g - DEPTH + 1))
                dve.wait_ge(to_trash_ready, g + 1)
                nc.vector.tensor_tensor(row_idx[:, b, :], to_trash[:, b, :], src_f[:, b, :], ALU.max
                                        ).then_inc(row_idx_ready, 1)

            def softplus(g, rnd, b):
                dve.wait_ge(log_ready, g + 1)
                nc.vector.scalar_tensor_tensor(soft[:, b % 2, :], ps_h[b % 2][:, :],
                                               b1_shifted[:, 0:1], clamped[:, b % 2, :],
                                               ALU.add, ALU.max).then_inc(soft_ready, 1)

            def multiply(g, rnd, b):
                dve.wait_ge(w_ready, g + 1)
                nc.vector.tensor_tensor(msg[:, b % 2, :], ps_w[b % 2][:, :], x_dst[:, b, :], ALU.mult
                                        ).then_inc(msg_ready, 1)

            def multiply_summed(g, rnd, b):
                dve.wait_ge(x_dst_ready, g + 1)
                multiply(g, rnd, b)

            def multiply_gathered(g, rnd, b):
                dve.wait_ge(gathered[b], 16 * TILES * (rnd + 1))
                multiply(g, rnd, b)

            by_flag(dve,
                    lambda: for_groups(dve, [(3, multiply_summed), (2, copy_src), (1, clamp),
                                             (0, split_rest), (2, make_same), (1, make_onehot),
                                             (2, find_trash), (1, split_low), (2, make_row_idx),
                                             (1, softplus)]),
                    lambda: for_groups(dve, [(3, multiply_gathered), (2, copy_src), (1, clamp),
                                             (2, make_same), (1, make_dst_idx), (2, find_trash),
                                             (2, make_row_idx), (1, softplus)]))

            def add_01(c):
                n, r = ln_size(c)
                zero, one = (part_sb[0:n, c % FIN, q, 0:r * feat] for q in range(2))
                dve.wait_ge(part_in[c % FIN], 16 * TILES * (c // FIN + 1))
                nc.vector.tensor_tensor(zero, zero, one, ALU.add).then_inc(pair01, 1)

            def statistics(c):
                n, r = ln_size(c)
                f = c % FIN
                dve.wait_ge(y_ready, c + 1)
                for k in range(r):
                    last = nc.vector.bn_stats(stats[0:n, f, k, :],
                                              part_sb[0:n, f, 0, k * feat:(k + 1) * feat])
                last.then_inc(stats_ready, 1)
                dve.wait_ge(stats_ready, c + 1)
                for k in range(r):
                    last = nc.vector.bn_aggr(mean_var[0:n, f, k, :], stats[0:n, f, k, :])
                last.then_inc(mean_var_ready, 1)

            def normalise(c):
                n, r = ln_size(c)
                f = c % FIN
                dve.wait_ge(std_ready, c + 1)
                nc.vector.reciprocal(rstd[0:n, f, 0:r], std[0:n, f, 0:r]).then_inc(rstd_ready, 1)
                dve.wait_ge(rstd_ready, c + 1)
                for k in range(r):
                    row = part_sb[0:n, f, 0, k * feat:(k + 1) * feat]
                    last = nc.vector.tensor_scalar(row, row, mean_var[0:n, f, k, 0:1],
                                                   rstd[0:n, f, k:k + 1], ALU.subtract, ALU.mult)
                last.then_inc(norm_ready, 1)

            for step in range(ln_chunks + 3):
                for late, part in ((0, add_01), (2, normalise), (1, statistics)):
                    if 0 <= step - late <= ln_chunks:
                        part(step - late)

        @block.tensor
        def _(pe):
            pe.wait_ge(dve_const, 5)
            pe.wait_ge(outside_ready, 1)
            nc.tensor.matmul(ps_c[0:1, 0:1], outside_any[:, :], ones_f[:, 0:1], start=True, stop=True
                             ).then_inc(flag_sum, 1)
            pe.wait_ge(diag_ready, 3)
            nc.tensor.matmul(ps_x[:, 0:groups], ones_f[:, :], base_diag[:, :], start=True, stop=True
                             ).then_inc(base_sum, 1)
            pe.wait_ge(weights_in, 64)
            pe.wait_ge(pool_const, 5)

            def transpose(g, rnd, b):
                pe.wait_ge(edge_in[b], 16 * (rnd + 1))
                if reaches(g, 2):
                    pe.wait_ge(edge_t_ready, g - 1)
                for q in range(TILES):
                    last = nc.tensor.transpose(ps_t[b % 2][:, q * P:(q + 1) * P],
                                               edge_sb[:, b, q, :], ident[:, :])
                last.then_inc(transposed, 1)

            def combine(g, rnd, b):
                pe.wait_ge(msg_ready, g + 1)
                pe.wait_ge(row_idx_ready, g + 1)
                if reaches(g, 1):
                    pe.wait_ge(summed_ready, g)
                for q in range(TILES):
                    last = nc.tensor.matmul(ps_c[:, q * P:(q + 1) * P], same[:, b % 2, q, :],
                                            msg[:, b % 2, q * P:(q + 1) * P], start=True, stop=True)
                last.then_inc(comb_ready, 1)

            def layer1(g, rnd, b):
                pe.wait_ge(edge_t_ready, g + 1)
                if reaches(g, 2):
                    pe.wait_ge(soft_ready, g - 1)
                nc.tensor.matmul(ps_h[b % 2][:, :], w1_sb[:, :], edge_t[:, b % 2, :],
                                 start=True, stop=True).then_inc(h_ready, 1)

            def sum_x_dst(g, rnd, b):
                pe.wait_ge(onehot_ready, g + 1)
                pe.wait_ge(x_low, g + 1)
                if reaches(g, 1):
                    pe.wait_ge(x_dst_ready, g)
                for q in range(TILES):
                    for k in range(SPLITS):
                        last = nc.tensor.matmul(ps_x[:, q * P:(q + 1) * P],
                                                onehot[:, b % 2, q::TILES], window[:, b, k, :],
                                                start=(k == 0), stop=(k == SPLITS - 1))
                last.then_inc(x_dst_summed, 1)

            def layer2(g, rnd, b):
                if reaches(g, 2):
                    pe.wait_ge(msg_ready, g - 1)
                if isinstance(g, int) and g == 0:
                    pe.wait_ge(b2_ready, TILES)
                nc.tensor.matmul(ps_w[b % 2][:, :], ones[:, :],
                                 b2_rows[:, :, :].rearrange("p q f -> p (q f)"),
                                 start=True, stop=False, skip_group_check=True)
                pe.wait_ge(soft_ready, g + 1)
                for q in range(TILES):
                    last = nc.tensor.matmul(ps_w[b % 2][:, q * P:(q + 1) * P],
                                            soft[:, b % 2, q * P:(q + 1) * P], w2_sb[:, :],
                                            start=False, stop=True, skip_group_check=True)
                last.then_inc(w_ready, 1)

            by_flag(pe,
                    lambda: for_groups(pe, [(0, transpose), (1, layer1), (2, sum_x_dst),
                                            (3, combine), (2, layer2)]),
                    lambda: for_groups(pe, [(0, transpose), (1, layer1), (3, combine),
                                            (2, layer2)]))


_INPUTS = ["x", "src", "dst", "edge_attr_128", "L0_gnn_W1", "L0_gnn_b1", "L0_gnn_W2", "L0_gnn_b2"]


def kernel(**inputs):
    from concourse import bacc
    from concourse.bass_utils import run_bass_kernel_spmd

    nc = bacc.Bacc("TRN2", target_bir_lowering=False, num_devices=1)
    arrays, views = {}, []
    for name in _INPUTS:
        a = np.ascontiguousarray(inputs[name])
        arrays[f"in_{name}"] = a
        views.append(nc.dram_tensor(f"in_{name}", a.shape, mybir.dt.from_np(a.dtype),
                                    kind="ExternalInput").ap())
    shape = np.asarray(inputs["x"]).shape
    views.append(nc.dram_tensor("out", shape, mybir.dt.float32, kind="ExternalOutput").ap())
    gnn_program(nc, *views)
    return run_bass_kernel_spmd(nc, [arrays], core_ids=[0]).results[0]["out"]
```
